# Optimizing a Trainium2 kernel written in Bass

```python
import numpy as np
import jax
import jax.numpy as jnp

def _softmax(x, axis=-1):
    return jax.nn.softmax(x, axis=axis)

def _gelu(x):
    return jax.nn.gelu(x, approximate=True)

def _silu(x):
    return jax.nn.silu(x)

def _sigmoid(x):
    return jax.nn.sigmoid(x)

def _layernorm(x, axis=-1, eps=1e-05):
    m = jnp.mean(x, axis=axis, keepdims=True)
    v = jnp.var(x, axis=axis, keepdims=True)
    return (x - m) / jnp.sqrt(v + eps)

def _scatter_add(tgt, idx, src, axis=0):
    return tgt.at[idx].add(src)

def _segment_sum(src, seg, n):
    return jax.ops.segment_sum(src, seg, n)
kernel_name = 'mk_prb_d2_jaxref_r8_e830f4'

def setup_inputs(seed: int=0):
    np.random.seed(seed)
    _w = jnp.asarray

    def _L0_attn_setup():
        import jax, jax.numpy as jnp
        import numpy as np
        E, H, W = (128, 16, 32)
        D = E // H

        def _rmsnorm(t, w):
            eps = jnp.finfo(t.dtype).eps
            return t * jax.lax.rsqrt(jnp.mean(t * t, axis=-1, keepdims=True) + eps) * w
        key = jax.random.key(seed)
        ks = jax.random.split(key, 11)
        B, T = (2, 256)
        s = 1.0 / np.sqrt(E)
        return {'x': jax.random.normal(ks[0], (B, T, E), jnp.float32), 'wq': jax.random.normal(ks[1], (E, E), jnp.float32) * s, 'bq': jnp.zeros((E,), jnp.float32), 'wk': jax.random.normal(ks[2], (E, E), jnp.float32) * s, 'bk': jnp.zeros((E,), jnp.float32), 'wv': jax.random.normal(ks[3], (E, E), jnp.float32) * s, 'bv': jnp.zeros((E,), jnp.float32), 'wo': jax.random.normal(ks[4], (E, E), jnp.float32) * s, 'bo': jnp.zeros((E,), jnp.float32), 'qn_w': jnp.ones((D,), jnp.float32), 'kn_w': jnp.ones((D,), jnp.float32)}
    _L0_attn_in = _L0_attn_setup()

    def _L0_ffn_setup():
        import jax, jax.numpy as jnp
        import numpy as np
        K = 32
        key = jax.random.key(seed)
        ks = jax.random.split(key, 9)
        B, S, D, O, E = (8, 256, 128, 128, 16)

        def xavier(k_, shape):
            fan_in, fan_out = (shape[-2], shape[-1])
            lim = (6.0 / (fan_in + fan_out)) ** 0.5
            return jax.random.uniform(k_, shape, jnp.float32, -lim, lim)
        return {'x': jax.random.normal(ks[0], (B, S, D), jnp.float32), 'Wg': xavier(ks[1], (D, E)), 'bg': jnp.zeros((E,), jnp.float32), 'w1': xavier(ks[2], (E, D, O)), 'b1': xavier(ks[3], (E, 1)), 'w2': xavier(ks[4], (E, O, O)), 'b2': xavier(ks[5], (E, 1)), 'w3': xavier(ks[6], (E, O, O)), 'b3': xavier(ks[7], (E, 1))}
    _L0_ffn_in = _L0_ffn_setup()

    def _L1_attn_setup():
        import jax, jax.numpy as jnp
        import numpy as np
        D_MODEL, D_STATE, D_CONV, EXPAND = (128, 16, 4, 2)
        D_INNER = EXPAND * D_MODEL
        DT_RANK = (D_MODEL + 15) // 16
        B_SZ, SEQ = (2, 128)

        def _mamba_dir(x, inW, convW, convB, xpW, dtW, dtB, Alog, Dp, outW):
            Bsz, L, _ = x.shape
            d_inner, d_state = Alog.shape
            dt_rank = xpW.shape[0] - 2 * d_state
            xz = jnp.einsum('bld,ed->ble', x, inW)
            xi, z = jnp.split(xz, 2, axis=-1)
            xc = jnp.swapaxes(xi, 1, 2)
            xc = jax.lax.conv_general_dilated(xc, convW, window_strides=(1,), padding=[(convW.shape[-1] - 1, 0)], feature_group_count=d_inner)
            xc = xc + convB[None, :, None]
            u = jax.nn.silu(jnp.swapaxes(xc, 1, 2))
            x_dbl = jnp.einsum('bld,ed->ble', u, xpW)
            dt, Bm, Cm = jnp.split(x_dbl, [dt_rank, dt_rank + d_state], axis=-1)
            delta = jax.nn.softplus(jnp.einsum('blr,dr->bld', dt, dtW) + dtB)
            A = -jnp.exp(Alog)

            def step(h, ins):
                d_t, B_t, C_t, u_t = ins
                dA = jnp.exp(d_t[:, :, None] * A)
                h = h * dA + (d_t * u_t)[:, :, None] * B_t[:, None, :]
                y_t = jnp.einsum('bdn,bn->bd', h, C_t)
                return (h, y_t)
            h0 = jnp.zeros((Bsz, d_inner, d_state), x.dtype)
            xs = (jnp.swapaxes(delta, 0, 1), jnp.swapaxes(Bm, 0, 1), jnp.swapaxes(Cm, 0, 1), jnp.swapaxes(u, 0, 1))
            _, ys = jax.lax.scan(step, h0, xs)
            y = jnp.swapaxes(ys, 0, 1)
            y = y + u * Dp
            y = y * jax.nn.silu(z)
            return jnp.einsum('bld,od->blo', y, outW)

        def _make_params(key, suffix):
            ks = jax.random.split(key, 10)
            s = 0.02
            p = {'inW' + suffix: jax.random.normal(ks[0], (2 * D_INNER, D_MODEL), jnp.float32) * s, 'convW' + suffix: jax.random.normal(ks[1], (D_INNER, 1, D_CONV), jnp.float32) * s, 'convB' + suffix: jnp.zeros((D_INNER,), jnp.float32), 'xpW' + suffix: jax.random.normal(ks[2], (DT_RANK + 2 * D_STATE, D_INNER), jnp.float32) * s, 'dtW' + suffix: jax.random.normal(ks[3], (D_INNER, DT_RANK), jnp.float32) * s, 'dtB' + suffix: jax.random.normal(ks[4], (D_INNER,), jnp.float32) * 0.1 - 4.0, 'Alog' + suffix: jnp.log(1.0 + jax.random.uniform(ks[5], (D_INNER, D_STATE), jnp.float32) * 15.0), 'Dp' + suffix: jnp.ones((D_INNER,), jnp.float32), 'outW' + suffix: jax.random.normal(ks[6], (D_MODEL, D_INNER), jnp.float32) * s}
            return p
        key = jax.random.key(seed)
        kx, kf, kb = jax.random.split(key, 3)
        inp = {'x': jax.random.normal(kx, (B_SZ, SEQ, D_MODEL), jnp.float32)}
        inp.update(_make_params(kf, '_f'))
        inp.update(_make_params(kb, '_b'))
        return inp
    _L1_attn_in = _L1_attn_setup()

    def _L1_ffn_setup():
        import jax, jax.numpy as jnp
        import numpy as np
        B, T, D, H = (4, 256, 128, 256)
        E, S, K = (8, 2, 2)

        def _swiglu_stacked(x, w1, b1, w2, b2, w3, b3):
            p1 = jnp.einsum('btd,ndh->nbth', x, w1) + b1[:, None, None, :]
            p2 = jnp.einsum('btd,ndh->nbth', x, w2) + b2[:, None, None, :]
            glu = jax.nn.silu(p1) * p2
            return jnp.einsum('nbth,nhd->nbtd', glu, w3) + b3[:, None, None, :]
        key = jax.random.key(seed)
        ks = jax.random.split(key, 10)
        s = 0.02
        return {'x': jax.random.normal(ks[0], (B, T, D), jnp.float32), 'gate_w': jax.random.normal(ks[1], (D, E), jnp.float32) * s, 'gate_b': jnp.zeros((E,), jnp.float32), 'rw1': jax.random.normal(ks[2], (E, D, H), jnp.float32) * s, 'rb1': jnp.zeros((E, H), jnp.float32), 'rw2': jax.random.normal(ks[3], (E, D, H), jnp.float32) * s, 'rb2': jnp.zeros((E, H), jnp.float32), 'rw3': jax.random.normal(ks[4], (E, H, D), jnp.float32) * s, 'rb3': jnp.zeros((E, D), jnp.float32), 'sw1': jax.random.normal(ks[5], (S, D, H), jnp.float32) * s, 'sb1': jnp.zeros((S, H), jnp.float32), 'sw2': jax.random.normal(ks[6], (S, D, H), jnp.float32) * s, 'sb2': jnp.zeros((S, H), jnp.float32), 'sw3': jax.random.normal(ks[7], (S, H, D), jnp.float32) * s, 'sb3': jnp.zeros((S, D), jnp.float32)}
    _L1_ffn_in = _L1_ffn_setup()
    _d = {'L0_attn_x': _L0_attn_in['x'], 'L0_attn_wq': _L0_attn_in['wq'], 'L0_attn_bq': _L0_attn_in['bq'], 'L0_attn_wk': _L0_attn_in['wk'], 'L0_attn_bk': _L0_attn_in['bk'], 'L0_attn_wv': _L0_attn_in['wv'], 'L0_attn_bv': _L0_attn_in['bv'], 'L0_attn_wo': _L0_attn_in['wo'], 'L0_attn_bo': _L0_attn_in['bo'], 'L0_attn_qn_w': _L0_attn_in['qn_w'], 'L0_attn_kn_w': _L0_attn_in['kn_w'], 'L0_ffn_Wg': _L0_ffn_in['Wg'], 'L0_ffn_bg': _L0_ffn_in['bg'], 'L0_ffn_w1': _L0_ffn_in['w1'], 'L0_ffn_b1': _L0_ffn_in['b1'], 'L0_ffn_w2': _L0_ffn_in['w2'], 'L0_ffn_b2': _L0_ffn_in['b2'], 'L0_ffn_w3': _L0_ffn_in['w3'], 'L0_ffn_b3': _L0_ffn_in['b3'], 'L1_attn_inW_f': _L1_attn_in['inW_f'], 'L1_attn_convW_f': _L1_attn_in['convW_f'], 'L1_attn_convB_f': _L1_attn_in['convB_f'], 'L1_attn_xpW_f': _L1_attn_in['xpW_f'], 'L1_attn_dtW_f': _L1_attn_in['dtW_f'], 'L1_attn_dtB_f': _L1_attn_in['dtB_f'], 'L1_attn_Alog_f': _L1_attn_in['Alog_f'], 'L1_attn_Dp_f': _L1_attn_in['Dp_f'], 'L1_attn_outW_f': _L1_attn_in['outW_f'], 'L1_attn_inW_b': _L1_attn_in['inW_b'], 'L1_attn_convW_b': _L1_attn_in['convW_b'], 'L1_attn_convB_b': _L1_attn_in['convB_b'], 'L1_attn_xpW_b': _L1_attn_in['xpW_b'], 'L1_attn_dtW_b': _L1_attn_in['dtW_b'], 'L1_attn_dtB_b': _L1_attn_in['dtB_b'], 'L1_attn_Alog_b': _L1_attn_in['Alog_b'], 'L1_attn_Dp_b': _L1_attn_in['Dp_b'], 'L1_attn_outW_b': _L1_attn_in['outW_b'], 'L1_ffn_gate_w': _L1_ffn_in['gate_w'], 'L1_ffn_gate_b': _L1_ffn_in['gate_b'], 'L1_ffn_rw1': _L1_ffn_in['rw1'], 'L1_ffn_rb1': _L1_ffn_in['rb1'], 'L1_ffn_rw2': _L1_ffn_in['rw2'], 'L1_ffn_rb2': _L1_ffn_in['rb2'], 'L1_ffn_rw3': _L1_ffn_in['rw3'], 'L1_ffn_rb3': _L1_ffn_in['rb3'], 'L1_ffn_sw1': _L1_ffn_in['sw1'], 'L1_ffn_sb1': _L1_ffn_in['sb1'], 'L1_ffn_sw2': _L1_ffn_in['sw2'], 'L1_ffn_sb2': _L1_ffn_in['sb2'], 'L1_ffn_sw3': _L1_ffn_in['sw3'], 'L1_ffn_sb3': _L1_ffn_in['sb3']}
    _x0 = _d['L0_attn_x']
    _d['L0_attn_x'] = jax.random.normal(jax.random.fold_in(jax.random.key(seed), 1), (8, 512, 128), dtype=_x0.dtype)
    del _x0
    return _d

def reference(L0_attn_x, L0_attn_wq, L0_attn_bq, L0_attn_wk, L0_attn_bk, L0_attn_wv, L0_attn_bv, L0_attn_wo, L0_attn_bo, L0_attn_qn_w, L0_attn_kn_w, L0_ffn_Wg, L0_ffn_bg, L0_ffn_w1, L0_ffn_b1, L0_ffn_w2, L0_ffn_b2, L0_ffn_w3, L0_ffn_b3, L1_attn_inW_f, L1_attn_convW_f, L1_attn_convB_f, L1_attn_xpW_f, L1_attn_dtW_f, L1_attn_dtB_f, L1_attn_Alog_f, L1_attn_Dp_f, L1_attn_outW_f, L1_attn_inW_b, L1_attn_convW_b, L1_attn_convB_b, L1_attn_xpW_b, L1_attn_dtW_b, L1_attn_dtB_b, L1_attn_Alog_b, L1_attn_Dp_b, L1_attn_outW_b, L1_ffn_gate_w, L1_ffn_gate_b, L1_ffn_rw1, L1_ffn_rb1, L1_ffn_rw2, L1_ffn_rb2, L1_ffn_rw3, L1_ffn_rb3, L1_ffn_sw1, L1_ffn_sb1, L1_ffn_sw2, L1_ffn_sb2, L1_ffn_sw3, L1_ffn_sb3):

    def _L0_attn_ref(x, wq, bq, wk, bk, wv, bv, wo, bo, qn_w, kn_w):
        import jax, jax.numpy as jnp
        import numpy as np
        E, H, W = (128, 16, 32)
        D = E // H

        def _rmsnorm(t, w):
            eps = jnp.finfo(t.dtype).eps
            return t * jax.lax.rsqrt(jnp.mean(t * t, axis=-1, keepdims=True) + eps) * w
        B, T, _ = x.shape
        q = (x @ wq + bq).reshape(B, T, H, D).transpose(0, 2, 1, 3)
        k = (x @ wk + bk).reshape(B, T, H, D).transpose(0, 2, 1, 3)
        v = (x @ wv + bv).reshape(B, T, H, D).transpose(0, 2, 1, 3)
        q = _rmsnorm(q, qn_w)
        k = _rmsnorm(k, kn_w)
        scores = jnp.einsum('bhqd,bhkd->bhqk', q, k) / jnp.sqrt(jnp.float32(D))
        row = jnp.arange(T)[:, None]
        col = jnp.arange(T)[None, :]
        invalid = (col > row) | (row - col >= W)
        neg_inf = jnp.float32(-jnp.inf)
        scores = jnp.where(invalid, neg_inf, scores)
        masked_attn = jnp.where(invalid, 0.0, jax.nn.softmax(scores, axis=-1))
        gene_means = jnp.mean(jax.nn.sigmoid(masked_attn), axis=-1)
        denom = gene_means + 0.5
        sum_inv = jnp.sum(1.0 / denom, axis=2, keepdims=True)
        fitness = 1.0 / (denom * sum_inv)
        scores = scores + jnp.log(fitness)[..., None]
        attn = jax.nn.softmax(scores, axis=-1)
        out = jnp.einsum('bhqk,bhkd->bhqd', attn, v)
        out = out.transpose(0, 2, 1, 3).reshape(B, T, E)
        return out @ wo + bo

    def _L0_ffn_ref(x, Wg, bg, w1, b1, w2, b2, w3, b3):
        import jax, jax.numpy as jnp
        import numpy as np
        K = 32
        B, S, D = x.shape
        E, _, O = w1.shape
        logits = jnp.einsum('bsd,de->bse', x, Wg) + bg
        probs = jax.nn.softmax(logits, axis=-2)
        pv = jnp.transpose(probs, (0, 2, 1))
        vals, idx = jax.lax.top_k(pv, K)
        bidx = jnp.arange(B)[:, None, None]
        tok = x[bidx, idx]
        b1b = b1[None, :, None, :]
        b2b = b2[None, :, None, :]
        b3b = b3[None, :, None, :]
        h = jax.nn.relu(jnp.einsum('bekd,edo->beko', tok, w1) + b1b)
        h = jax.nn.relu(jnp.einsum('bekd,edo->beko', h, w2) + b2b)
        h = jnp.einsum('bekd,edo->beko', h, w3) + b3b
        out = h * vals[..., None]
        outputs = jnp.zeros((B, S, O), x.dtype).at[bidx, idx].add(out)
        return outputs

    def _L1_attn_ref(x, inW_f, convW_f, convB_f, xpW_f, dtW_f, dtB_f, Alog_f, Dp_f, outW_f, inW_b, convW_b, convB_b, xpW_b, dtW_b, dtB_b, Alog_b, Dp_b, outW_b):
        import jax, jax.numpy as jnp
        import numpy as np
        D_MODEL, D_STATE, D_CONV, EXPAND = (128, 16, 4, 2)
        D_INNER = EXPAND * D_MODEL
        DT_RANK = (D_MODEL + 15) // 16
        B_SZ, SEQ = (2, 128)

        def _mamba_dir(x, inW, convW, convB, xpW, dtW, dtB, Alog, Dp, outW):
            Bsz, L, _ = x.shape
            d_inner, d_state = Alog.shape
            dt_rank = xpW.shape[0] - 2 * d_state
            xz = jnp.einsum('bld,ed->ble', x, inW)
            xi, z = jnp.split(xz, 2, axis=-1)
            xc = jnp.swapaxes(xi, 1, 2)
            xc = jax.lax.conv_general_dilated(xc, convW, window_strides=(1,), padding=[(convW.shape[-1] - 1, 0)], feature_group_count=d_inner)
            xc = xc + convB[None, :, None]
            u = jax.nn.silu(jnp.swapaxes(xc, 1, 2))
            x_dbl = jnp.einsum('bld,ed->ble', u, xpW)
            dt, Bm, Cm = jnp.split(x_dbl, [dt_rank, dt_rank + d_state], axis=-1)
            delta = jax.nn.softplus(jnp.einsum('blr,dr->bld', dt, dtW) + dtB)
            A = -jnp.exp(Alog)

            def step(h, ins):
                d_t, B_t, C_t, u_t = ins
                dA = jnp.exp(d_t[:, :, None] * A)
                h = h * dA + (d_t * u_t)[:, :, None] * B_t[:, None, :]
                y_t = jnp.einsum('bdn,bn->bd', h, C_t)
                return (h, y_t)
            h0 = jnp.zeros((Bsz, d_inner, d_state), x.dtype)
            xs = (jnp.swapaxes(delta, 0, 1), jnp.swapaxes(Bm, 0, 1), jnp.swapaxes(Cm, 0, 1), jnp.swapaxes(u, 0, 1))
            _, ys = jax.lax.scan(step, h0, xs)
            y = jnp.swapaxes(ys, 0, 1)
            y = y + u * Dp
            y = y * jax.nn.silu(z)
            return jnp.einsum('bld,od->blo', y, outW)

        def _make_params(key, suffix):
            ks = jax.random.split(key, 10)
            s = 0.02
            p = {'inW' + suffix: jax.random.normal(ks[0], (2 * D_INNER, D_MODEL), jnp.float32) * s, 'convW' + suffix: jax.random.normal(ks[1], (D_INNER, 1, D_CONV), jnp.float32) * s, 'convB' + suffix: jnp.zeros((D_INNER,), jnp.float32), 'xpW' + suffix: jax.random.normal(ks[2], (DT_RANK + 2 * D_STATE, D_INNER), jnp.float32) * s, 'dtW' + suffix: jax.random.normal(ks[3], (D_INNER, DT_RANK), jnp.float32) * s, 'dtB' + suffix: jax.random.normal(ks[4], (D_INNER,), jnp.float32) * 0.1 - 4.0, 'Alog' + suffix: jnp.log(1.0 + jax.random.uniform(ks[5], (D_INNER, D_STATE), jnp.float32) * 15.0), 'Dp' + suffix: jnp.ones((D_INNER,), jnp.float32), 'outW' + suffix: jax.random.normal(ks[6], (D_MODEL, D_INNER), jnp.float32) * s}
            return p
        y_fwd = _mamba_dir(x, inW_f, convW_f, convB_f, xpW_f, dtW_f, dtB_f, Alog_f, Dp_f, outW_f)
        xb = jnp.flip(x, axis=1)
        y_bwd = jnp.flip(_mamba_dir(xb, inW_b, convW_b, convB_b, xpW_b, dtW_b, dtB_b, Alog_b, Dp_b, outW_b), axis=1)
        return 0.5 * (y_fwd + y_bwd)

    def _L1_ffn_ref(x, gate_w, gate_b, rw1, rb1, rw2, rb2, rw3, rb3, sw1, sb1, sw2, sb2, sw3, sb3):
        import jax, jax.numpy as jnp
        import numpy as np
        B, T, D, H = (4, 256, 128, 256)
        E, S, K = (8, 2, 2)

        def _swiglu_stacked(x, w1, b1, w2, b2, w3, b3):
            p1 = jnp.einsum('btd,ndh->nbth', x, w1) + b1[:, None, None, :]
            p2 = jnp.einsum('btd,ndh->nbth', x, w2) + b2[:, None, None, :]
            glu = jax.nn.silu(p1) * p2
            return jnp.einsum('nbth,nhd->nbtd', glu, w3) + b3[:, None, None, :]
        scores = jax.nn.softmax(x @ gate_w + gate_b, axis=-1)
        weights, indices = jax.lax.top_k(scores, K)
        routed_all = _swiglu_stacked(x, rw1, rb1, rw2, rb2, rw3, rb3)
        out_bted = jnp.transpose(routed_all, (1, 2, 0, 3))
        gathered = jnp.take_along_axis(out_bted, indices[..., None], axis=2)
        routed = jnp.sum(weights[..., None] * gathered, axis=2)
        shared = _swiglu_stacked(x, sw1, sb1, sw2, sb2, sw3, sb3).mean(axis=0)
        return shared + routed
    x = L0_attn_x
    xn = _layernorm(x, axis=-1)
    x = x + _L0_attn_ref(xn, L0_attn_wq, L0_attn_bq, L0_attn_wk, L0_attn_bk, L0_attn_wv, L0_attn_bv, L0_attn_wo, L0_attn_bo, L0_attn_qn_w, L0_attn_kn_w) + _L0_ffn_ref(xn, L0_ffn_Wg, L0_ffn_bg, L0_ffn_w1, L0_ffn_b1, L0_ffn_w2, L0_ffn_b2, L0_ffn_w3, L0_ffn_b3)
    xn = _layernorm(x, axis=-1)
    x = x + _L1_attn_ref(xn, L1_attn_inW_f, L1_attn_convW_f, L1_attn_convB_f, L1_attn_xpW_f, L1_attn_dtW_f, L1_attn_dtB_f, L1_attn_Alog_f, L1_attn_Dp_f, L1_attn_outW_f, L1_attn_inW_b, L1_attn_convW_b, L1_attn_convB_b, L1_attn_xpW_b, L1_attn_dtW_b, L1_attn_dtB_b, L1_attn_Alog_b, L1_attn_Dp_b, L1_attn_outW_b) + _L1_ffn_ref(xn, L1_ffn_gate_w, L1_ffn_gate_b, L1_ffn_rw1, L1_ffn_rb1, L1_ffn_rw2, L1_ffn_rb2, L1_ffn_rw3, L1_ffn_rb3, L1_ffn_sw1, L1_ffn_sb1, L1_ffn_sw2, L1_ffn_sb2, L1_ffn_sw3, L1_ffn_sb3)
    return x

_drawn_inputs = setup_inputs


def setup_inputs(seed=0):
    import zlib

    import numpy as np

    out = dict(_drawn_inputs(seed))
    spreads = {'L0_attn_bq': (0.0, 0.39),
     'L0_attn_bk': (0.0, 0.622),
     'L0_attn_bv': (0.0, 0.1),
     'L0_attn_bo': (0.0, 0.1),
     'L0_attn_qn_w': (1.0, 0.566),
     'L0_attn_kn_w': (1.0, 0.6),
     'L0_ffn_bg': (0.0, 2.0),
     'L1_attn_convB_f': (0.0, 0.8),
     'L1_attn_Dp_f': (1.0, 0.6),
     'L1_attn_convB_b': (0.0, 0.8),
     'L1_attn_Dp_b': (1.0, 0.6),
     'L1_ffn_gate_b': (0.0, 0.698),
     'L1_ffn_rb1': (0.0, 0.8),
     'L1_ffn_rb2': (0.0, 0.8),
     'L1_ffn_rb3': (0.0, 2.0),
     'L1_ffn_sb1': (0.0, 0.8),
     'L1_ffn_sb2': (0.0, 0.8),
     'L1_ffn_sb3': (0.0, 2.0)}
    factors = {'L0_ffn_Wg': 4.525,
     'L0_ffn_w1': 7.958,
     'L0_ffn_b1': 8.0,
     'L0_ffn_w2': 6.537,
     'L0_ffn_b2': 8.0,
     'L0_ffn_w3': 4.746,
     'L0_ffn_b3': 28.068,
     'L1_attn_inW_f': 8.0,
     'L1_attn_convW_f': 8.0,
     'L1_attn_xpW_f': 8.0,
     'L1_attn_dtW_f': 8.0,
     'L1_attn_dtB_f': 8.0,
     'L1_attn_Alog_f': 8.0,
     'L1_attn_outW_f': 8.0,
     'L1_attn_inW_b': 8.0,
     'L1_attn_convW_b': 8.0,
     'L1_attn_xpW_b': 8.0,
     'L1_attn_dtW_b': 8.0,
     'L1_attn_dtB_b': 8.0,
     'L1_attn_Alog_b': 8.0,
     'L1_attn_outW_b': 8.0,
     'L1_ffn_gate_w': 3.013,
     'L1_ffn_rw1': 8.0,
     'L1_ffn_rw2': 8.0,
     'L1_ffn_rw3': 8.0,
     'L1_ffn_sw1': 8.0,
     'L1_ffn_sw2': 8.0,
     'L1_ffn_sw3': 8.0}
    for name, (base, spread) in spreads.items():
        noise = np.random.default_rng([zlib.crc32(name.encode()), seed]).standard_normal(out[name].shape)
        drawn = base * np.exp(spread * noise) if base else spread * noise
        out[name] = jnp.asarray(drawn.astype(out[name].dtype))
    for name, factor in factors.items():
        out[name] = (out[name] * factor).astype(out[name].dtype)
    return out
```

```python
from contextlib import ExitStack

import numpy as np
import concourse.bass as bass
from concourse import mybir

F32 = mybir.dt.float32
BF16 = mybir.dt.bfloat16
U32 = mybir.dt.uint32
ALU = mybir.AluOpType
ACT = mybir.ActivationFunctionType
AX = mybir.AxisListType

P = 128
NB, T, E0 = 8, 512, 128
NC = T // P
NH = 16
HD = E0 // NH
BW = 32
KW = 2 * BW
NQ = T // BW
XP = 3 * BW
NE, TOPK = 16, 32
NS, DI, KC, NX = 16, 256, 4, 40
NS2 = 2 * NS
NG = 2 * NS
RING = 4
LAG = 3
NR, NX1, DH = 8, 10, 256
V_STEPS, P_STEPS = 25, 6
LN_EPS = 1e-5
RMS_EPS = float(np.finfo(np.float32).eps)


def constants():
    q = np.arange(P) % BW
    k = np.arange(KW)
    seen = (k[None] > q[:, None]) & (k[None] <= q[:, None] + BW)
    no_past = seen & ~((np.arange(P) < BW)[:, None] & (k < BW)[None])
    band = np.where(np.stack([seen, no_past], 1), 0.0, MASKED).astype(np.float32)
    head = (np.arange(P) // HD) % 4
    return {
        "c_ident": np.eye(P, dtype=np.float32),
        "c_band": band,
        "c_row0": (np.arange(P, dtype=np.float32) // NE * T)[:, None],
        "c_sel": np.tile(np.eye(NS2, dtype=np.float32), (3, 1)),
        "c_iota": np.tile(np.arange(NR, dtype=np.float32), (P, 1)),
        "c_head_of_4": (head[:, None] == np.arange(4)[None]).astype(np.float32),
    }


MASKED = -1e30


def layouts(a):
    blocks = lambda x: np.ascontiguousarray(x.reshape(2, P, -1).transpose(1, 0, 2))
    t = {}
    for s in "fb":
        w = {k: a[f"L1_attn_{k}_{s}"] for k in ("inW", "convW", "convB", "xpW", "dtW", "dtB", "Alog", "Dp", "outW")}
        t["t_in_w_" + s] = np.ascontiguousarray(w["inW"].T)
        t["t_conv_w_" + s] = blocks(w["convW"][:, 0])
        t["t_conv_b_" + s] = blocks(w["convB"])[:, :, 0]
        bcd = np.concatenate([w["xpW"][NX - NS2:], w["xpW"][:NX - NS2]])
        t["t_x_w_" + s] = blocks(bcd.T)
        t["t_dt_w_" + s] = np.ascontiguousarray(w["dtW"].T)
        t["t_dt_b_" + s] = blocks(w["dtB"])[:, :, 0]
        t["t_a_log_" + s] = blocks(w["Alog"])
        t["t_d_p_" + s] = blocks(w["Dp"])[:, :, 0]
        t["t_out_w_" + s] = blocks(w["outW"].T)
    for n in (1, 2):
        b = np.concatenate([a[f"L1_ffn_rb{n}"], a[f"L1_ffn_sb{n}"]])
        t[f"t_b{n}"] = b.reshape(NX1, 2, P).transpose(2, 0, 1)
    return {k: np.ascontiguousarray(v) for k, v in t.items()}


def alone(eng, s_pass):
    eng.sem_inc(s_pass, 1)


class Banks:

    def __init__(self, sem, name, tiles, uses):
        n = len(tiles)
        assert len(uses) % n == 0 and len(set(uses)) == len(uses)
        self.per = len(uses) // n
        self.fill = [sem(f"{name}_fill{k}") for k in range(n)]
        self.empty = [sem(f"{name}_empty{k}") for k in range(n)]
        self.tiles = tiles
        self.at = {key: (m % n, m // n) for m, key in enumerate(uses)}

    def bank(self, *key):
        return self.tiles[self.at[key][0]]

    def wait_filled(self, eng, i, *key):
        k, n = self.at[key]
        eng.wait_ge(self.fill[k], i * self.per + n + 1)

    def wait_free(self, eng, i, *key):
        k, n = self.at[key]
        eng.wait_ge(self.empty[k], i * self.per + n)

    def wait_emptied(self, eng, i, *key):
        k, n = self.at[key]
        eng.wait_ge(self.empty[k], i * self.per + n + 1)

    def filled(self, ins, *key):
        ins.then_inc(self.fill[self.at[key][0]], 1)

    def emptied(self, ins, *key):
        ins.then_inc(self.empty[self.at[key][0]], 1)


def attention_phase(nc, a, scr):
    U = 2
    ctx = ExitStack()
    with ctx:
        def sb(name, shape, dt=F32):
            return ctx.enter_context(nc.sbuf_tensor(name, shape, dt))

        def sem(name):
            return ctx.enter_context(nc.semaphore(name))

        ident = sb("a_ident", [P, P])
        w_qk = sb("a_w_qk", [P, 2 * E0])
        w_v = sb("a_w_v", [P, E0])
        w_o = sb("a_w_o", [P, E0])
        w_g = sb("a_w_g", [P, NE])
        b_g = sb("a_b_g", [NE, 1])
        b_qk = sb("a_b_qk", [P, 2 * E0])
        b_v = sb("a_b_v", [P, E0])
        b_o = sb("a_b_o", [P, E0])
        qn_b = sb("a_qn_b", [P, HD])
        kn_b = sb("a_kn_b", [P, HD])
        qk_w = sb("a_qk_w", [P, HD])
        band = sb("a_band", [P, 2, KW])
        head_of_4 = sb("a_head_of_4", [P, 4])
        xt = sb("a_xt", [P, U, NC, E0])
        xb = sb("a_xb", [P, U, NC, E0])
        xn = sb("a_xn", [P, U, NC, E0])
        stats = sb("a_stats", [P, U, NC, 6])
        mv = sb("a_mv", [P, U, NC, 2])
        var = sb("a_var", [P, U, NC])
        lnv = sb("a_lnv", [P, U, NC])
        rstd = sb("a_rstd", [P, U, NC])
        xnT = sb("a_xnT", [P, U, XP + T])
        lg = sb("a_lg", [NE, U, T])
        qk = sb("a_qk", [P, U, NC, 2 * E0])
        sq = sb("a_sq", [P, U, NC, 2 * E0])
        ms = sb("a_ms", [P, U, NC * 2 * NH])
        mse = sb("a_mse", [P, U, NC * 2 * NH])
        lms = sb("a_lms", [P, U, NC * 2 * NH])
        rs = sb("a_rs", [P, U, NC * 2 * NH])
        qn = sb("a_qn", [P, U, NC, 2 * E0])
        qT = sb("a_qT", [P, U, T])
        kblk = sb("a_kblk", [P, U, 4, BW + T])
        prob = sb("a_prob", [P, U, 2, NH, KW])
        mx = sb("a_mx", [P, U, 2 * NH])
        pT = sb("a_pT", [P, 2, 4, P])
        vblk = sb("a_vblk", [P, U, NQ, NH // 2, 2 * (HD + 1)])
        rc = sb("a_rc", [P, U, 2, NH])
        att = sb("a_att", [P, U, NC, E0])
        attT = sb("a_attT", [P, U, T])
        x1 = sb("a_x1", [P, U, NC, E0])

        ps_s = ctx.enter_context(nc.psum_tensor("a_ps_s", [P, 4, 512], F32))
        ps_g = [ctx.enter_context(nc.psum_tensor(f"a_ps_g{n}", [P, 512], F32)) for n in range(2)]
        ps_h = [ctx.enter_context(nc.psum_tensor(f"a_ps_h{n}", [P, 512], F32)) for n in range(2)]

        order = [(0, 0), (1, 0), (0, 1), (1, 1)]
        g_uses = [("xnT", u) for u in range(U)] + [("lg", u) for u in range(U)]
        g_uses += [(n, u) for u in range(U) for n in ("qT", "kT")]
        g_uses += [("pT", u, cp, k) for u, cp in order for k in range(4)]
        g_uses += [("attT", u) for u in range(U)] + [("wo", u) for u in range(U)]
        h_uses = [("v", u, n) for u in range(U) for n in range(5)] + [("pv", u, cp) for u, cp in order]
        G = Banks(sem, "a_g", ps_g, g_uses)
        H = Banks(sem, "a_h", ps_h, h_uses)

        def pool_of(key):
            return H if key[0] in ("v", "pv") else G

        def bank(*key):
            return pool_of(key).bank(*key)

        def fill_wait(eng, i, *key):
            pool_of(key).wait_filled(eng, i, *key)

        def free_wait(eng, i, *key):
            pool_of(key).wait_free(eng, i, *key)

        def evac_wait(eng, i, *key):
            pool_of(key).wait_emptied(eng, i, *key)

        def filled(ins, *key):
            pool_of(key).filled(ins, *key)

        def emptied(ins, *key):
            pool_of(key).emptied(ins, *key)

        s_pass = sem("a_pass")
        s_const = sem("a_const")
        s_zero = sem("a_zero")
        s_qkw = sem("a_qkw")
        s_x = [sem(f"a_x{u}") for u in range(U)]
        s_xn_out = [sem(f"a_xn_out{u}") for u in range(U)]
        s_lg_out = [sem(f"a_lg_out{u}") for u in range(U)]
        s_x1_out = [sem(f"a_x1_out{u}") for u in range(U)]
        s_stats = sem("a_stats_ready")
        s_mv = sem("a_mv_ready")
        s_var = sem("a_var_ready")
        s_ln = sem("a_ln_ready")
        s_rstd = sem("a_rstd_ready")
        s_xn = sem("a_xn_ready")
        s_xb = sem("a_xb_ready")
        s_qk_fill = sem("a_qk_filled")
        s_qk = sem("a_qk_ready")
        s_sq = sem("a_sq_ready")
        s_ms = sem("a_ms_ready")
        s_mse = sem("a_mse_ready")
        s_lms = sem("a_lms_ready")
        s_rs = sem("a_rs_ready")
        s_qn0 = sem("a_qn_scaled")
        s_qn = sem("a_qn_ready")
        s_sc = sem("a_scores_filled")
        s_masked = sem("a_scores_masked")
        s_mx = sem("a_max_ready")
        s_sub = sem("a_max_subtracted")
        s_p = sem("a_prob_ready")
        s_pv = sem("a_pT_used")
        s_rc = sem("a_rc_ready")

        n_iter = NB // U
        x_v = a["L0_attn_x"].rearrange("b (c p) e -> b p c e", p=P)
        xn_v = scr["xn"].rearrange("(b c p) e -> b p c e", b=NB, p=P)
        x1_v = scr["x1"].rearrange("(b c p) e -> b p c e", b=NB, p=P)
        lg_v = scr["lg"].rearrange("(b e) t -> b e t", b=NB)
        loads = [
            (ident[:, :], a["c_ident"]), (band[:, :, :], a["c_band"]), (head_of_4[:, :], a["c_head_of_4"]),
            (w_qk[:, 0:E0], a["L0_attn_wq"]), (w_qk[:, E0:], a["L0_attn_wk"]), (w_v[:, :], a["L0_attn_wv"]),
            (w_o[:, :], a["L0_attn_wo"]), (w_g[:, :], a["L0_ffn_Wg"]),
            (b_g[:, :], a["L0_ffn_bg"].unsqueeze(1)),
            (b_qk[:, 0:E0], a["L0_attn_bq"].partition_broadcast(P)),
            (b_qk[:, E0:], a["L0_attn_bk"].partition_broadcast(P)),
            (b_v[:, :], a["L0_attn_bv"].partition_broadcast(P)),
            (b_o[:, :], a["L0_attn_bo"].partition_broadcast(P)),
            (qn_b[:, :], a["L0_attn_qn_w"].partition_broadcast(P)),
            (kn_b[:, :], a["L0_attn_kn_w"].partition_broadcast(P)),
        ]
        consts_in = 16 * len(loads)
        block = ctx.enter_context(nc.Block())

        @block.sync
        def _(sp):
            for u in range(U):
                sp.dma_start(xt[:, u], x_v[u]).then_inc(s_x[u], 16)
            for dst, src in loads:
                sp.dma_start(dst, src).then_inc(s_const, 16)
            with sp.Fori(0, n_iter) as i:
                for u in range(U):
                    sp.wait_ge(s_xn, i * U + u + 1)
                    sp.dma_start(xn_v[i * U + u], xn[:, u]).then_inc(s_xn_out[u], 16)
                for u in range(U):
                    evac_wait(sp, i, "lg", u)
                    sp.dma_start(lg_v[i * U + u], lg[:, u]).then_inc(s_lg_out[u], 16)
                ahead = (i + 1) % n_iter
                for u in range(U):
                    sp.wait_ge(s_xb, i * U + u + 1)
                    sp.dma_start(xt[:, u], x_v[ahead * U + u]).then_inc(s_x[u], 16)
                for u in range(U):
                    evac_wait(sp, i, "wo", u)
                    sp.dma_start(x1_v[i * U + u], x1[:, u]).then_inc(s_x1_out[u], 16)
            for u in range(U):
                sp.wait_ge(s_x[u], 16 * (n_iter + 1))
                sp.wait_ge(s_xn_out[u], 16 * n_iter)
                sp.wait_ge(s_lg_out[u], 16 * n_iter)
                sp.wait_ge(s_x1_out[u], 16 * n_iter)

        @block.gpsimd
        def _(pool):
            pool.memset(xnT[:, :, 0:XP], 0.0).then_inc(s_zero, 1)
            pool.memset(kblk[:, :, :, 0:BW], 0.0).then_inc(s_zero, 1)
            pool.memset(vblk[:, :, :, :, :], 0.0).then_inc(s_zero, 1)
            pool.wait_ge(s_zero, 3)
            for u in range(U):
                pool.memset(vblk[0:64, u, :, :, HD:HD + 1], 1.0).then_inc(s_zero, 1)
                pool.memset(vblk[64:P, u, :, :, 2 * HD + 1:], 1.0).then_inc(s_zero, 1)
        zeroed = 3 + 2 * U

        @block.scalar
        def _(act):
            act.preload_act_table_set("natural_log_exp_and_others")
            act.wait_ge(s_const, consts_in)
            act.wait_ge(s_zero, zeroed)
            with act.Fori(0, n_iter) as i:
                for u in range(U):
                    n = i * U + u + 1
                    act.wait_ge(s_var, n)
                    act.activation(lnv[:, u], var[:, u], ACT.Ln).then_inc(s_ln, 1)
                    act.wait_ge(s_ln, n)
                    act.activation(rstd[:, u], lnv[:, u], ACT.Exp, scale=-0.5).then_inc(s_rstd, 1)
                for u in range(U):
                    fill_wait(act, i, "xnT", u)
                    emptied(act.copy(xnT[:, u, XP:], bank("xnT", u)[:, :]), "xnT", u)
                for u in range(U):
                    fill_wait(act, i, "lg", u)
                    act.wait_ge(s_lg_out[u], i * 16)
                    emptied(act.activation(lg[:, u], bank("lg", u)[0:NE, :], ACT.Identity, bias=b_g[:, :]), "lg", u)
                for u in range(U):
                    act.wait_ge(s_qk, i * U + u + 1)
                    act.activation(sq[:, u], qk[:, u], ACT.Square).then_inc(s_sq, 1)
                for u in range(U):
                    n = i * U + u + 1
                    act.wait_ge(s_mse, n)
                    act.activation(lms[:, u], mse[:, u], ACT.Ln).then_inc(s_lms, 1)
                    act.wait_ge(s_lms, n)
                    act.activation(rs[:, u], lms[:, u], ACT.Exp, scale=-0.5).then_inc(s_rs, 1)
                for u in range(U):
                    fill_wait(act, i, "qT", u)
                    emptied(act.copy(qT[:, u], bank("qT", u)[:, :]), "qT", u)
                    fill_wait(act, i, "kT", u)
                    for h in range(4):
                        last = act.activation(kblk[:, u, h, BW:], bank("kT", u)[:, :], ACT.Copy,
                                              scale=head_of_4[:, h:h + 1])
                    emptied(last, "kT", u)
                for m, (u, cp) in enumerate(order):
                    act.wait_ge(s_sub, i * 4 + m + 1)
                    act.activation(prob[:, u], prob[:, u], ACT.Exp).then_inc(s_p, 1)
                    for k in range(4):
                        fill_wait(act, i, "pT", u, cp, k)
                        if k != 1:
                            act.wait_ge(s_pv, i * 12 + 3 * m + max(k - 1, 0))
                        elif m:
                            fill_wait(act, i, "pv", *order[m - 1])
                        else:
                            act.wait_ge(H.fill[H.at[("pv", *order[3])][0]], i * H.per)
                        emptied(act.copy(pT[:, k % 2], bank("pT", u, cp, k)[:, :]
                                         .rearrange("p (h q) -> p h q", h=4)), "pT", u, cp, k)
                for u in range(U):
                    fill_wait(act, i, "attT", u)
                    emptied(act.copy(attT[:, u], bank("attT", u)[:, :]), "attT", u)

        @block.vector
        def _(dve):
            dve.wait_ge(s_const, consts_in)
            dve.wait_ge(s_zero, zeroed)
            dve.scalar_tensor_tensor(qk_w[:, :], qn_b[:, :], HD ** -0.5, kn_b[:, :], ALU.mult, ALU.mult)\
               .then_inc(s_qkw, 1)
            dve.wait_ge(s_qkw, 1)
            with dve.Fori(0, n_iter) as i:
                for u in range(U):
                    dve.wait_ge(s_x[u], i * 16 + 16)
                    for c in range(NC):
                        last = dve.bn_stats(stats[:, u, c], xt[:, u, c])
                    last.then_inc(s_stats, 1)
                    dve.wait_ge(s_stats, i * U + u + 1)
                    alone(dve, s_pass)
                    for c in range(NC):
                        last = dve.bn_aggr(mv[:, u, c], stats[:, u, c])
                    last.then_inc(s_mv, 1)
                    dve.wait_ge(s_mv, i * U + u + 1)
                    dve.tensor_scalar(var[:, u], mv[:, u, :, 1], LN_EPS, None, ALU.add).then_inc(s_var, 1)
                for u in range(U):
                    dve.wait_ge(s_rstd, i * U + u + 1)
                    dve.wait_ge(s_xn_out[u], i * 16)
                    for c in range(NC):
                        last = dve.tensor_scalar(xn[:, u, c], xt[:, u, c], mv[:, u, c, 0:1], rstd[:, u, c:c + 1],
                                                 ALU.subtract, ALU.mult)
                    last.then_inc(s_xn, 1)
                    dve.tensor_tensor(xb[:, u], xt[:, u], b_o[:, :].unsqueeze(1).broadcast_to([P, NC, E0]),
                                      ALU.add).then_inc(s_xb, 1)
                for u in range(U):
                    dve.wait_ge(s_qk_fill, i * U + u + 1)
                    bias = b_qk[:, :].unsqueeze(1).broadcast_to([P, 2, 2 * E0])
                    for h in range(2):
                        last = dve.tensor_tensor(qk[:, u, 2 * h:2 * h + 2],
                                                 ps_s[:, 2 * u + h].rearrange("p (c n) -> p c n", c=2), bias, ALU.add)
                    last.then_inc(s_qk, 1)
                for u in range(U):
                    for n in range(5):
                        fill_wait(dve, i, "v", u, n)
                        for hh in range(2):
                            q = slice(64 * hh, 64 * hh + 64)
                            w0 = 2 if n == 0 and hh == 0 else 0
                            w1 = 2 if n == 4 else 4
                            if n == 4 and hh == 1:
                                continue
                            src = bank("v", u, n)[q, :].rearrange("p (w m h d) -> p w m h d", w=4, m=NH // 2, h=2)
                            bias = b_v[q, :].rearrange("p (m h d) -> p m h d", m=NH // 2, h=2)[:, :, hh]
                            to = 4 * n - 2 + 2 * hh
                            last = dve.tensor_tensor(
                                vblk[q, u, to + w0:to + w1, :, hh * (HD + 1):hh * (HD + 1) + HD],
                                src[:, w0:w1, :, hh], bias.unsqueeze(1).broadcast_to([64, w1 - w0, NH // 2, HD]), ALU.add)
                        emptied(last, "v", u, n)
                for u in range(U):
                    dve.wait_ge(s_sq, i * U + u + 1)
                    dve.tensor_reduce(ms[:, u], sq[:, u].rearrange("p c (h d) -> p (c h) d", d=HD), AX.X, ALU.add)\
                       .then_inc(s_ms, 1)
                    dve.wait_ge(s_ms, i * U + u + 1)
                    dve.tensor_scalar(mse[:, u], ms[:, u], 1.0 / HD, RMS_EPS, ALU.mult, ALU.add).then_inc(s_mse, 1)
                for u in range(U):
                    dve.wait_ge(s_rs, i * U + u + 1)
                    dve.tensor_tensor(qn[:, u].rearrange("p c (h d) -> p (c h) d", d=HD),
                                      qk[:, u].rearrange("p c (h d) -> p (c h) d", d=HD),
                                      rs[:, u].unsqueeze(2).broadcast_to([P, NC * 2 * NH, HD]), ALU.mult)\
                       .then_inc(s_qn0, 1)
                    dve.wait_ge(s_qn0, i * U + u + 1)
                    q = qn[:, u, :, 0:E0].rearrange("p c (h d) -> p c h d", d=HD)
                    dve.tensor_tensor(q, q, qk_w[:, :].unsqueeze(1).unsqueeze(1).broadcast_to([P, NC, NH, HD]),
                                      ALU.mult).then_inc(s_qn, 1)

                def softmax(m):
                    u, cp = order[m]
                    n = i * 4 + m + 1
                    dve.wait_ge(s_sc, n)
                    if cp == 1:
                        fill_wait(dve, i, "pT", u, 0, 3)
                    for cc in range(2):
                        first = 1 if cp == 0 and cc == 0 else 0
                        mask = band[:, first].unsqueeze(1).unsqueeze(1).broadcast_to([P, 4, 4, KW])
                        last = dve.tensor_tensor(
                            prob[:, u, cc].rearrange("p (g h) k -> p g h k", g=4),
                            ps_s[:, :, 256 * cc:256 * cc + 256].rearrange("p g (h k) -> p g h k", h=4), mask, ALU.add)
                    last.then_inc(s_masked, 1)
                    dve.wait_ge(s_masked, n)
                    flat = prob[:, u].rearrange("p c h k -> p (c h) k")
                    dve.tensor_reduce(mx[:, u], flat, AX.X, ALU.max).then_inc(s_mx, 1)
                    dve.wait_ge(s_mx, n)
                    dve.tensor_tensor(flat, flat, mx[:, u].unsqueeze(2).broadcast_to([P, 2 * NH, KW]),
                                      ALU.subtract).then_inc(s_sub, 1)

                def normalise(m):
                    u, cp = order[m]
                    fill_wait(dve, i, "pv", u, cp)
                    o = bank("pv", u, cp)[:, 0:2 * NH * (HD + 1)].rearrange("p (c h d) -> p c h d", c=2, h=NH)
                    dve.reciprocal(rc[:, u], o[:, :, :, HD]).then_inc(s_rc, 1)
                    dve.wait_ge(s_rc, i * 4 + m + 1)
                    emptied(dve.tensor_tensor(
                        att[:, u, 2 * cp:2 * cp + 2].rearrange("p c (h d) -> p c h d", d=HD), o[:, :, :, 0:HD],
                        rc[:, u].unsqueeze(3).broadcast_to([P, 2, NH, HD]), ALU.mult), "pv", u, cp)

                softmax(0)
                softmax(1)
                for m in range(4):
                    if m + 2 < 4:
                        softmax(m + 2)
                    normalise(m)
                for u in range(U):
                    fill_wait(dve, i, "wo", u)
                    dve.wait_ge(s_x1_out[u], i * 16)
                    dve.wait_ge(s_xb, i * U + U)
                    last = dve.tensor_tensor(x1[:, u], bank("wo", u)[:, :].rearrange("p (c n) -> p c n", c=NC),
                                             xb[:, u], ALU.add)
                    emptied(last, "wo", u)

        @block.tensor
        def _(pe):
            pe.wait_ge(s_const, consts_in)
            pe.wait_ge(s_zero, zeroed)
            with pe.Fori(0, n_iter) as i:
                for u in range(U):
                    pe.wait_ge(s_xn, i * U + u + 1)
                    free_wait(pe, i, "xnT", u)
                    for c in range(NC):
                        last = pe.transpose(bank("xnT", u)[:, P * c:P * c + P], xn[:, u, c], ident[:, :])
                    filled(last, "xnT", u)
                for u in range(U):
                    evac_wait(pe, i, "xnT", u)
                    free_wait(pe, i, "lg", u)
                    filled(pe.matmul(bank("lg", u)[0:NE, :], w_g[:, :], xnT[:, u, XP:], start=True, stop=True),
                           "lg", u)
                pe.wait_ge(s_masked, i * 4)
                for u in range(U):
                    for c in range(NC):
                        out = ps_s[:, 2 * u + c // 2, 256 * (c % 2):256 * (c % 2) + 256]
                        last = pe.matmul(out, xnT[:, u, XP + P * c:XP + P * c + P], w_qk[:, :], start=True, stop=True)
                    last.then_inc(s_qk_fill, 1)
                for u in range(U):
                    for n in range(5):
                        free_wait(pe, i, "v", u, n)
                        for w in range(2 if n == 4 else 4):
                            t0 = XP - BW + BW * (4 * n - 2 + w)
                            keys = KW if n == 4 else 2 * KW
                            last = pe.matmul(bank("v", u, n)[0:keys, P * w:P * w + P], xnT[:, u, t0:t0 + keys],
                                             w_v[:, :], start=True, stop=True)
                        filled(last, "v", u, n)
                for u in range(U):
                    pe.wait_ge(s_qn, i * U + u + 1)
                    for name, off in (("qT", 0), ("kT", E0)):
                        free_wait(pe, i, name, u)
                        for c in range(NC):
                            last = pe.transpose(bank(name, u)[:, P * c:P * c + P], qn[:, u, c, off:off + E0], ident[:, :])
                        filled(last, name, u)

                def scores(m):
                    u, cp = order[m]
                    evac_wait(pe, i, "qT", u)
                    evac_wait(pe, i, "kT", u)
                    if m == 0:
                        pe.wait_ge(s_qk, i * U + U)
                    else:
                        pe.wait_ge(s_masked, i * 4 + m)
                    alone(pe, s_pass)
                    for cc in range(2):
                        for j in range(4):
                            t0 = P * (2 * cp + cc) + BW * j
                            for g in range(4):
                                q = slice(32 * g, 32 * g + 32)
                                last = pe.matmul(ps_s[32 * j:32 * j + 32, g, 256 * cc:256 * cc + 256],
                                                 qT[q, u, t0:t0 + BW], kblk[q, u, :, t0:t0 + KW],
                                                 start=True, stop=True)
                    last.then_inc(s_sc, 1)

                def turn(m, k):
                    u, cp = order[m]
                    free_wait(pe, i, "pT", u, cp, k)
                    pe.wait_ge(s_p, i * 4 + m + 1)
                    for n in range(4):
                        h = 8 * (k % 2) + 2 * n
                        last = pe.transpose(bank("pT", u, cp, k)[:, P * n:P * n + P],
                                            prob[:, u, k // 2, h:h + 2].rearrange("p h k -> p (h k)"), ident[:, :])
                    filled(last, "pT", u, cp, k)

                def p_v(m, k):
                    u, cp = order[m]
                    evac_wait(pe, i, "pT", u, cp, k)
                    if k == 0:
                        free_wait(pe, i, "pv", u, cp)
                    for n in range(4):
                        pair = 4 * (k % 2) + n
                        col = (k // 2) * NH * (HD + 1) + pair * 2 * (HD + 1)
                        for j in range(4):
                            w = 4 * (2 * cp + k // 2) + j
                            last = pe.matmul(bank("pv", u, cp)[32 * j:32 * j + 32, col:col + 2 * (HD + 1)],
                                             pT[:, k % 2, n, 32 * j:32 * j + 32], vblk[:, u, w, pair, :],
                                             start=True, stop=True)
                    if k < 3:
                        last.then_inc(s_pv, 1)
                    else:
                        filled(last, "pv", u, cp)

                scores(0)
                scores(1)
                for m in range(4):
                    if m + 2 < 4:
                        scores(m + 2)
                    for k in range(4):
                        turn(m, k)
                        if k:
                            p_v(m, k - 1)
                    p_v(m, 3)
                for u in range(U):
                    free_wait(pe, i, "attT", u)
                    evac_wait(pe, i, "pv", u, 1)
                    for c in range(NC):
                        last = pe.transpose(bank("attT", u)[:, P * c:P * c + P], att[:, u, c], ident[:, :])
                    filled(last, "attT", u)
                for u in range(U):
                    free_wait(pe, i, "wo", u)
                    evac_wait(pe, i, "attT", u)
                    for c in range(NC):
                        last = pe.matmul(bank("wo", u)[:, P * c:P * c + P], attT[:, u, P * c:P * c + P], w_o[:, :],
                                         start=True, stop=True)
                    filled(last, "wo", u)


def expert_phase(nc, a, scr):
    U = 2
    ctx = ExitStack()
    with ctx:
        def sb(name, shape, dt=F32):
            return ctx.enter_context(nc.sbuf_tensor(name, shape, dt))

        def sem(name):
            return ctx.enter_context(nc.semaphore(name))

        ident = sb("b_ident", [P, P])
        row0 = sb("b_row0", [P, 1])
        bias = sb("b_bias", [P, 3, NE])
        lg = sb("b_lg", [P, T])
        ex = sb("b_ex", [P, T])
        pr = sb("b_pr", [P, 2, T])
        mx = sb("b_mx", [P, 1])
        nmx = sb("b_nmx", [P, 1])
        ssum = sb("b_ssum", [P, 1])
        rsum = sb("b_rsum", [P, 1])
        vals = sb("b_vals", [P, TOPK])
        idx = sb("b_idx", [P, TOPK], U32)
        rowf = sb("b_rowf", [P, TOPK])
        row_at = sb("b_row_at", [P, NE, 2], U32)
        val_at = sb("b_val_at", [P, NE, 2])
        row_now = sb("b_row_now", [P, U, 2], U32)
        val_now = sb("b_val_now", [P, U, 2])
        bias_now = sb("b_bias_now", [P, U, 3])
        w = sb("b_w", [P, U, 3, E0])
        xg = sb("b_xg", [P, U, 2, E0])
        xgT = sb("b_xgT", [P, U, 2 * P])
        h1 = sb("b_h1", [P, U, 2 * P])
        h2 = sb("b_h2", [P, U, 2 * P])
        y = sb("b_y", [P, U, 2, E0])
        ps_t = [ctx.enter_context(nc.psum_tensor(f"b_ps_t{n}", [P, 512], F32)) for n in range(2)]
        ps_x = [ctx.enter_context(nc.psum_tensor(f"b_ps_x{u}", [P, 512], F32)) for u in range(U)]
        ps_1 = [ctx.enter_context(nc.psum_tensor(f"b_ps_1{u}", [P, 512], F32)) for u in range(U)]
        ps_2 = [ctx.enter_context(nc.psum_tensor(f"b_ps_2{u}", [P, 512], F32)) for u in range(U)]

        s_pass = sem("b_pass")
        s_const = sem("b_const")
        s_w = [sem(f"b_w{u}") for u in range(U)]
        s_g = sem("b_gate_step")
        s_exp = sem("b_exp_ready")
        s_turned = sem("b_slots_turned")
        s_row = sem("b_row_at_ready")
        s_row_now = sem("b_row_now_ready")
        s_bias_now = sem("b_bias_now_ready")
        s_val_now = sem("b_val_now_ready")
        s_xg = [sem(f"b_xg{u}") for u in range(U)]
        s_xt_fill = sem("b_xgT_filled")
        s_xt = sem("b_xgT_ready")
        s_1_fill = sem("b_h1_filled")
        s_1 = sem("b_h1_ready")
        s_2_fill = sem("b_h2_filled")
        s_2 = sem("b_h2_ready")
        s_3_fill = sem("b_y_filled")
        s_y = sem("b_y_ready")
        s_out = sem("b_y_added")

        n_iter = NE // U
        loads = [(lg[:, :], scr["lg"]), (ident[:, :], a["c_ident"]), (row0[:, :], a["c_row0"])]
        loads += [(bias[:, n, :], a[f"L0_ffn_b{n + 1}"].rearrange("e o -> (e o)").partition_broadcast(P)) for n in range(3)]
        w_v = [a[f"L0_ffn_w{n + 1}"] for n in range(3)]
        block = ctx.enter_context(nc.Block())

        @block.sync
        def _(sp):
            for dst, src in loads:
                sp.dma_start(dst, src).then_inc(s_const, 16)
            with sp.Fori(0, n_iter) as i:
                for u in range(U):
                    sp.wait_ge(s_3_fill, i * U)
                    for n in range(3):
                        sp.dma_start(w[:, u, n], w_v[n][i * U + u]).then_inc(s_w[u], 16)

        @block.vector
        def _(dve):
            step = [0]

            def then(ins):
                step[0] += 1
                ins.then_inc(s_g, 1)
                dve.wait_ge(s_g, step[0])

            dve.wait_ge(s_const, 16 * len(loads))
            then(dve.tensor_reduce(mx[:, :], lg[:, :], AX.X, ALU.max))
            then(dve.tensor_scalar(nmx[:, :], mx[:, :], -1.0, None, ALU.mult))
            dve.wait_ge(s_exp, 1)
            then(dve.reciprocal(rsum[:, :], ssum[:, :]))
            then(dve.tensor_scalar(pr[:, 0], ex[:, :], rsum[:, :], None, ALU.mult))
            for r in range(TOPK // 8):
                now = slice(8 * r, 8 * r + 8)
                then(dve.max(vals[:, now], pr[:, r % 2]))
                then(dve.max_index(idx[:, now], vals[:, now], pr[:, r % 2]))
                if r + 1 < TOPK // 8:
                    then(dve.match_replace(pr[:, (r + 1) % 2], vals[:, now], pr[:, r % 2], -1.0))
            then(dve.tensor_copy(rowf[:, :], idx[:, :]))
            then(dve.tensor_scalar(rowf[:, :], rowf[:, :], row0[:, :], None, ALU.add))
            dve.wait_ge(s_turned, 1)
            for b4 in range(4):
                q = slice(32 * b4, 32 * b4 + 32)
                for src, dst in ((ps_t[0], row_at), (ps_t[1], val_at)):
                    turned = src[0:TOPK, 0:P].rearrange("k (h b e) -> k e h b", h=2, b=4)[:, :, :, b4]
                    last = dve.tensor_copy(dst[q, :, :], turned)
            last.then_inc(s_row, 1)
            dve.wait_ge(s_row, 1)
            with dve.Fori(0, n_iter) as i:
                for u in range(U):
                    dve.wait_ge(s_y, i * U)
                    dve.tensor_copy(val_now[:, u, :], val_at[:, i * U + u]).then_inc(s_val_now, 1)
                for u in range(U):
                    dve.wait_ge(s_3_fill, i * U + u + 1)
                    dve.wait_ge(s_val_now, i * U + U)
                    dve.wait_ge(s_bias_now, i * U + U)
                    dve.wait_ge(s_out, i * 64)
                    for h in range(2):
                        last = dve.tensor_scalar(y[:, u, h], ps_x[u][:, P * h:P * h + P], bias_now[:, u, 2:3],
                                                 val_now[:, u, h:h + 1], ALU.add, ALU.mult)
                    last.then_inc(s_y, 1)
        gate_steps = 4 + 3 * (TOPK // 8) - 1 + 2

        @block.gpsimd
        def _(pool):
            pool.wait_ge(s_row, 1)
            with pool.Fori(0, n_iter) as i:
                for u in range(U):
                    pool.wait_ge(s_xg[u], i * 32)
                    pool.tensor_copy(row_now[:, u, :], row_at[:, i * U + u]).then_inc(s_row_now, 1)
                for u in range(U):
                    pool.wait_ge(s_row_now, i * U + U)
                    pool.wait_ge(s_xt_fill, i * U)
                    alone(pool, s_pass)
                    for h in range(2):
                        pool.indirect_dma_start(
                            out=xg[:, u, h], out_offset=None, in_=scr["xn"],
                            in_offset=bass.IndirectOffsetOnAxis(ap=row_now[:, u, h:h + 1], axis=0)).then_inc(s_xg[u], 16)
                for u in range(U):
                    pool.wait_ge(s_y, i * U + u + 1)
                    alone(pool, s_pass)
                    for h in range(2):
                        pool.indirect_dma_start(
                            out=scr["x1"], out_offset=bass.IndirectOffsetOnAxis(ap=row_now[:, u, h:h + 1], axis=0),
                            in_=y[:, u, h], in_offset=None, compute_op=ALU.add).then_inc(s_out, 16)
                        pool.wait_ge(s_out, i * 64 + 32 * u + 16 * h + 16)
                        alone(pool, s_pass)

        @block.scalar
        def _(act):
            act.wait_ge(s_g, 2)
            act.activation(ex[:, :], lg[:, :], ACT.Exp, bias=nmx[:, :], accum_out=ssum[:, :]).then_inc(s_exp, 1)
            with act.Fori(0, n_iter) as i:
                for u in range(U):
                    act.wait_ge(s_y, i * U)
                    act.copy(bias_now[:, u, :], bias[:, :, i * U + u]).then_inc(s_bias_now, 1)
                for u in range(U):
                    act.wait_ge(s_xt_fill, i * U + u + 1)
                    act.copy(xgT[:, u], ps_x[u][:, 0:2 * P]).then_inc(s_xt, 1)
                act.wait_ge(s_bias_now, i * U + U)
                for u in range(U):
                    act.wait_ge(s_1_fill, i * U + u + 1)
                    act.activation(h1[:, u], ps_1[u][:, 0:2 * P], ACT.Relu, bias=bias_now[:, u, 0:1]).then_inc(s_1, 1)
                for u in range(U):
                    act.wait_ge(s_2_fill, i * U + u + 1)
                    act.activation(h2[:, u], ps_2[u][:, 0:2 * P], ACT.Relu, bias=bias_now[:, u, 1:2]).then_inc(s_2, 1)

        @block.tensor
        def _(pe):
            pe.wait_ge(s_g, gate_steps)
            pe.transpose(ps_t[0][0:TOPK, 0:P], rowf[:, :], ident[:, :])
            pe.transpose(ps_t[1][0:TOPK, 0:P], vals[:, :], ident[:, :]).then_inc(s_turned, 1)
            with pe.Fori(0, n_iter) as i:
                for u in range(U):
                    pe.wait_ge(s_xg[u], i * 32 + 32)
                    pe.wait_ge(s_y, i * U)
                    for h in range(2):
                        last = pe.transpose(ps_x[u][:, P * h:P * h + P], xg[:, u, h], ident[:, :])
                    last.then_inc(s_xt_fill, 1)
                for u in range(U):
                    pe.wait_ge(s_xt, i * U + u + 1)
                    pe.wait_ge(s_w[u], i * 48 + 48)
                    pe.matmul(ps_1[u][:, 0:2 * P], w[:, u, 0], xgT[:, u], start=True, stop=True).then_inc(s_1_fill, 1)
                for u in range(U):
                    pe.wait_ge(s_1, i * U + u + 1)
                    pe.matmul(ps_2[u][:, 0:2 * P], w[:, u, 1], h1[:, u], start=True, stop=True).then_inc(s_2_fill, 1)
                for u in range(U):
                    pe.wait_ge(s_2, i * U + u + 1)
                    for h in range(2):
                        last = pe.matmul(ps_x[u][:, P * h:P * h + P], h2[:, u, P * h:P * h + P], w[:, u, 2],
                                         start=True, stop=True)
                    last.then_inc(s_3_fill, 1)


def layer1_phase(nc, a, scr, out):
    ctx = ExitStack()
    with ctx:
        def sb(name, shape, dt=F32):
            return ctx.enter_context(nc.sbuf_tensor(name, shape, dt))

        def sem(name):
            return ctx.enter_context(nc.semaphore(name))

        def ps(name):
            return ctx.enter_context(nc.psum_tensor(name, [P, 512], F32))

        ident = sb("m_ident_sb", [P, P])
        sel_f = sb("m_sel_f", [3 * NS2, NS2])
        sel = sb("m_sel", [3 * NS2, NS2, P], BF16)
        iota = sb("m_iota_sb", [P, NR])
        in_w = sb("m_in_w", [P, 2, 2 * DI])
        conv_w = sb("m_conv_w", [P, 2, 2, KC])
        conv_b = sb("m_conv_b", [P, 2, 2])
        x_w = sb("m_x_w", [P, 2, 2, NX])
        dt_w = sb("m_dt_w", [NX, 2, DI])
        dt_b = sb("m_dt_b", [P, 2, 2])
        a_log = sb("m_a_log", [P, 2, 2, NS])
        a_neg = sb("m_a_neg", [P, 2, 2, NS])
        d_p = sb("m_d_p", [P, 2, 2])
        out_w = sb("m_out_w", [P, 2, 2, E0])
        gate_w = sb("m_gate_w", [P, NR])
        gate_b = sb("m_gate_b", [P, NR])
        w1 = sb("m_w1", [P, NX1, DH])
        w2 = sb("m_w2", [P, NX1, DH])
        w3 = sb("m_w3", [P, NX1, 2, E0])
        b1 = sb("m_b1", [P, NX1, 2])
        b2 = sb("m_b2", [P, NX1, 2])
        b3 = sb("m_b3", [NX1, E0])

        xs = sb("m_xs", [P, NC, E0])
        xn = sb("m_xn", [P, NC, E0])
        stats = sb("m_stats", [P, NC, 6])
        mv = sb("m_mv", [P, NC, 2])
        var = sb("m_var", [P, NC])
        lnv = sb("m_lnv", [P, NC])
        rstd = sb("m_rstd", [P, NC])
        xnT = sb("m_xnT", [P, T])
        gl = sb("m_gl", [P, NC, NR])
        gm = sb("m_gm", [P, NC])
        ge = sb("m_ge", [P, NC, NR])
        gs = sb("m_gs", [P, NC])
        gr = sb("m_gr", [P, NC])
        gp = sb("m_gp", [P, NC, NR])
        top = sb("m_top", [P, NC, NR])
        top_i = sb("m_top_i", [P, NC, NR], U32)
        top_f = sb("m_top_f", [P, NC, NR])
        g1 = sb("m_g1", [P, NC, NR])
        g2 = sb("m_g2", [P, NC, NR])
        g = sb("m_g", [P, NC, NR])
        g_t = sb("m_g_t", [P, NC, NX1])
        gT = sb("m_gT", [NX1, T])
        xi = sb("m_xi", [P, 2, 2, T + 2 * (KC - 1)])
        uu = sb("m_uu", [P, 2, 2, T])
        sz = sb("m_sz", [P, 2, 2, T])
        xd = sb("m_xd", [NX, 2, T])
        bc = sb("m_bc", [3 * NS2, 2, T], BF16)
        bc_m = sb("m_bc_m", [NS2, 2, T], BF16)
        bc_l = sb("m_bc_l", [NS2, 2, T], BF16)
        bc_r = sb("m_bc_r", [NS2, 2, T])
        dl = sb("m_dl", [P, 2, T])
        sp_e = sb("m_sp_e", [P, 2, T])
        sp_w = sb("m_sp_w", [P, 2, T])
        sp_l = sb("m_sp_l", [P, 2, T])
        delta = sb("m_delta", [P, 2, 2, T])
        du = sb("m_du", [P, 2, 2, T])
        dA = sb("m_dA", [P, RING, 2, T])
        dBu = sb("m_dBu", [P, 2, 2, T])
        h = sb("m_h", [P, RING, 2, T])
        c_n = sb("m_c_n", [P, RING, T])
        hc = sb("m_hc", [P, RING, 2, T])
        s1 = h[:, 0]
        glu = hc[:, 0:2]
        cv = dBu[:, 0]
        acc = sb("m_acc", [P, NC, E0])
        yo = sb("m_yo", [P, NC, E0])

        ps_y = [ps(f"m_ps_y{n}") for n in range(2)]
        ps_b = [ps(f"m_ps_b{n}") for n in range(2)]
        ps_c = ps("m_ps_c")
        shared = [NR, NR + 1]
        uses = [("xnT",), ("gate",)]
        uses += [("in", d, k) for d in range(2) for k in range(4)]
        for e in shared:
            uses += [(p, e, k) for k in range(2) for p in ("p1", "p2")]
        uses += [("gT",), ("xd", 0), ("out", "shared"), ("xd", 1)]
        for e in range(NR):
            uses += [(p, e, k) for k in range(2) for p in ("p1", "p2")]
            if e:
                uses += [("out", e - 1)]
        uses += [("out", NR - 1)] + [("dl", d, k) for d in range(2) for k in range(2)]
        G = Banks(sem, "m_g", [ps(f"m_ps_g{n}") for n in range(3)], uses)

        s_const = sem("m_const")
        s_setup = sem("m_setup")
        s_sel = sem("m_sel_ready")
        s_a = sem("m_a_exp")
        s_x = sem("m_x_loaded")
        s_out = sem("m_out_stored")
        s_v = sem("m_vector_step")
        s_p = sem("m_pool_step")
        s_var = sem("m_var_ready")
        s_lnv = sem("m_lnv_ready")
        s_rstd = sem("m_rstd_ready")
        s_xn = sem("m_xn_ready")
        s_gm = sem("m_gate_less_max")
        s_ge = sem("m_gate_exp")
        s_gt = sem("m_gates_ready")
        s_cv = sem("m_conv_ready")
        s_u = sem("m_u_ready")
        s_lo = sem("m_bc_split")
        s_bc = sem("m_bc_ready")
        s_dl = sem("m_dl_ready")
        s_abs = sem("m_abs_ready")
        s_e = sem("m_e_ready")
        s_l = sem("m_l_ready")
        s_delta = sem("m_delta_ready")
        s_du = sem("m_du_ready")
        s_b_fill = sem("m_b_filled")
        s_c_fill = sem("m_c_filled")
        s_c = sem("m_c_ready")
        s_dA = sem("m_dA_ready")
        s_dBu = sem("m_dBu_ready")
        s_h = sem("m_h_ready")
        s_hc = sem("m_hc_ready")
        s_ysum = sem("m_ysum_done")
        s_y = sem("m_y_ready")
        s_o_fill = sem("m_o_filled")
        s_yo = sem("m_yo_ready")
        s_pass = sem("m_pass")

        x_v = scr["x1"].rearrange("(b c p) e -> b p c e", b=NB, p=P)
        out_v = out.rearrange("b (c p) e -> b p c e", p=P)
        loads = [
            (ident[:, :], a["c_ident"]), (sel_f[:, :], a["c_sel"]), (iota[:, :], a["c_iota"]),
            (gate_w[:, :], a["L1_ffn_gate_w"]), (gate_b[:, :], a["L1_ffn_gate_b"].partition_broadcast(P)),
            (w1[:, 0:NR, :], a["L1_ffn_rw1"].rearrange("e d h -> d e h")),
            (w1[:, NR:, :], a["L1_ffn_sw1"].rearrange("e d h -> d e h")),
            (w2[:, 0:NR, :], a["L1_ffn_rw2"].rearrange("e d h -> d e h")),
            (w2[:, NR:, :], a["L1_ffn_sw2"].rearrange("e d h -> d e h")),
            (w3[:, 0:NR, :, :], a["L1_ffn_rw3"].rearrange("e (k p) d -> p e k d", p=P)),
            (w3[:, NR:, :, :], a["L1_ffn_sw3"].rearrange("e (k p) d -> p e k d", p=P)),
            (b3[0:NR, :], a["L1_ffn_rb3"]), (b3[NR:, :], a["L1_ffn_sb3"]),
            (b1[:, :, :], a["t_b1"]), (b2[:, :, :], a["t_b2"]),
        ]
        for d, s in enumerate("fb"):
            loads += [
                (in_w[:, d, :], a["t_in_w_" + s]), (conv_w[:, d], a["t_conv_w_" + s]), (conv_b[:, d], a["t_conv_b_" + s]),
                (x_w[:, d], a["t_x_w_" + s]), (dt_w[NS2:NX, d, :], a["t_dt_w_" + s]), (dt_b[:, d], a["t_dt_b_" + s]),
                (a_log[:, d], a["t_a_log_" + s]), (d_p[:, d], a["t_d_p_" + s]), (out_w[:, d], a["t_out_w_" + s]),
            ]
        consts_in = 16 * len(loads)

        def n_steps(eng, step):
            for d in range(2):
                for k in range(4):
                    step(d, k, k, NS * d + k)
                with eng.Fori(1, NS // 4) as m:
                    for k in range(4):
                        step(d, k, m * 4 + k, m * 4 + (NS * d + k))

        def lowered(g, by, i):
            return max(g - by, 0) if isinstance(g, int) else g - by

        block = ctx.enter_context(nc.Block())

        @block.sync
        def _(sp):
            sp.dma_start(xs[:, :, :], x_v[0]).then_inc(s_x, 16)
            for dst, src in loads:
                sp.dma_start(dst, src).then_inc(s_const, 16)
            with sp.Fori(0, NB) as i:
                G.wait_emptied(sp, i, "out", "shared")
                sp.dma_start(xs[:, :, :], x_v[(i + 1) % NB]).then_inc(s_x, 16)
                sp.wait_ge(s_yo, i + 1)
                sp.dma_start(out_v[i], yo[:, :, :]).then_inc(s_out, 16)
            sp.wait_ge(s_x, 16 * (NB + 1))
            sp.wait_ge(s_out, 16 * NB)

        @block.vector
        def _(dve):
            dve.wait_ge(s_const, consts_in)
            dve.tensor_copy(sel[:, :, :], sel_f[:, :].unsqueeze(2).broadcast_to([3 * NS2, NS2, P])).then_inc(s_sel, 1)
            dve.wait_ge(s_setup, 2)
            per = V_STEPS
            with dve.Fori(0, NB) as i:
                done = [0]

                def then(ins):
                    done[0] += 1
                    ins.then_inc(s_v, 1)
                    dve.wait_ge(s_v, i * per + done[0])

                dve.wait_ge(s_x, i * 16 + 16)
                for c in range(NC):
                    last = dve.bn_stats(stats[:, c], xs[:, c])
                then(last)
                alone(dve, s_pass)
                for c in range(NC):
                    last = dve.bn_aggr(mv[:, c], stats[:, c])
                then(last)
                dve.tensor_scalar(var[:, :], mv[:, :, 1], LN_EPS, None, ALU.add).then_inc(s_var, 1)
                dve.wait_ge(s_rstd, i + 1)
                for c in range(NC):
                    last = dve.tensor_scalar(xn[:, c], xs[:, c], mv[:, c, 0:1], rstd[:, c:c + 1], ALU.subtract, ALU.mult)
                last.then_inc(s_xn, 1)

                G.wait_filled(dve, i, "gate")
                last = dve.tensor_tensor(gl[:, :, :], G.bank("gate")[:, 0:NC * NR].rearrange("p (c e) -> p c e", c=NC),
                                         gate_b[:, :].unsqueeze(1).broadcast_to([P, NC, NR]), ALU.add)
                G.emptied(last, "gate")
                G.wait_emptied(dve, i, "gate")
                then(dve.tensor_reduce(gm[:, :], gl[:, :, :], AX.X, ALU.max))
                dve.tensor_tensor(gp[:, :, :], gl[:, :, :], gm[:, :].unsqueeze(2).broadcast_to([P, NC, NR]),
                                  ALU.subtract).then_inc(s_gm, 1)
                dve.wait_ge(s_ge, i + 1)
                then(dve.tensor_reduce(gs[:, :], ge[:, :, :], AX.X, ALU.add))
                then(dve.reciprocal(gr[:, :], gs[:, :]))
                then(dve.tensor_tensor(gp[:, :, :], ge[:, :, :], gr[:, :].unsqueeze(2).broadcast_to([P, NC, NR]), ALU.mult))
                alone(dve, s_pass)
                for c in range(NC):
                    last = dve.max(top[:, c], gp[:, c])
                then(last)
                alone(dve, s_pass)
                for c in range(NC):
                    last = dve.max_index(top_i[:, c], top[:, c], gp[:, c])
                then(last)
                then(dve.tensor_copy(top_f[:, :, :], top_i[:, :, :]))
                for c in range(NC):
                    dve.tensor_scalar(g1[:, c], iota[:, :], top_f[:, c, 0:1], top[:, c, 0:1], ALU.is_equal, ALU.mult)
                    last = dve.tensor_scalar(g2[:, c], iota[:, :], top_f[:, c, 1:2], top[:, c, 1:2], ALU.is_equal, ALU.mult)
                then(last)
                then(dve.tensor_tensor(g[:, :, :], g1[:, :, :], g2[:, :, :], ALU.add))
                dve.tensor_scalar(g_t[:, :, 0:NR], g[:, :, :], 2.0, None, ALU.mult).then_inc(s_gt, 1)

                def conv(d):
                    for k in range(2):
                        G.wait_emptied(dve, i, "in", d, k)
                    dve.wait_ge(s_u, i * 2 + d)
                    for tap in range(KC - 1, -1, -1):
                        off = tap if d == 0 else 2 * (KC - 1) - tap
                        for k in range(2):
                            src, w = xi[:, d, k, off:off + T], conv_w[:, d, k, tap:tap + 1]
                            if tap == KC - 1:
                                last = dve.tensor_scalar(cv[:, k], src, w, conv_b[:, d, k:k + 1], ALU.mult, ALU.add)
                            else:
                                last = dve.scalar_tensor_tensor(cv[:, k], src, w, cv[:, k], ALU.mult, ALU.add)
                        if tap:
                            then(last)
                    last.then_inc(s_cv, 1)

                def glus(e, order):
                    for k in range(2):
                        G.wait_emptied(dve, i, "p1", e, k)
                        G.wait_filled(dve, i, "p2", e, k)
                        last = dve.scalar_tensor_tensor(glu[:, order % 2, k], G.bank("p2", e, k)[:, :], b2[:, e, k:k + 1],
                                                        s1[:, k], ALU.add, ALU.mult)
                        G.emptied(last, "p2", e, k)

                def add(e):
                    G.wait_filled(dve, i, "out", e)
                    G.wait_emptied(dve, i, "out", e - 1 if e else "shared")
                    for c in range(NC):
                        last = dve.scalar_tensor_tensor(acc[:, c], G.bank("out", e)[:, P * c:P * c + P], g[:, c, e:e + 1],
                                                        acc[:, c], ALU.mult, ALU.add)
                    G.emptied(last, "out", e)

                conv(0)
                glus(shared[0], 0)
                conv(1)
                glus(shared[1], 1)
                G.wait_filled(dve, i, "out", "shared")
                G.emptied(dve.scalar_tensor_tensor(
                    acc[:, :, :], G.bank("out", "shared")[:, :].rearrange("p (c n) -> p c n", c=NC), 0.5, xs[:, :, :],
                    ALU.mult, ALU.add), "out", "shared")
                for e in range(NR):
                    glus(e, 2 + e)
                    if e:
                        add(e - 1)
                add(NR - 1)

                for d in range(2):
                    dve.wait_ge(s_e, i * 2 + d + 1)
                    then(dve.tensor_scalar(sp_w[:, :, :], sp_e[:, :, :], 1.0, -1.0, ALU.add, ALU.add))
                    then(dve.tensor_tensor(sp_w[:, :, :], sp_w[:, :, :], sp_e[:, :, :], ALU.subtract))
                    dve.wait_ge(s_l, i * 2 + d + 1)
                    then(dve.tensor_tensor(sp_w[:, :, :], sp_l[:, :, :], sp_w[:, :, :], ALU.subtract))
                    dve.scalar_tensor_tensor(delta[:, d].rearrange("p k t -> p (k t)"), dl[:, :, :].rearrange("p k t -> p (k t)"),
                                             0.0, sp_w[:, :, :].rearrange("p k t -> p (k t)"), ALU.max, ALU.add)\
                       .then_inc(s_delta, 1)
                    dve.wait_ge(s_delta, i * 2 + d + 1)
                    dve.tensor_tensor(du[:, d], delta[:, d], uu[:, d], ALU.mult).then_inc(s_du, 1)
                dve.wait_ge(s_du, i * 2 + 2)

                def scan(d, k, g):
                    dve.wait_ge(s_dA, i * NG + (g + 1))
                    dve.wait_ge(s_dBu, i * NG + (g + 1))
                    free_steps(dve, s_hc, g, RING)
                    for b in range(2):
                        t = slice(None, None, 1 if d == 0 else -1)
                        last = dve.tensor_tensor_scan(h[:, k % RING, b][:, t], dA[:, k % RING, b][:, t],
                                                      dBu[:, k % 2, b][:, t], 0.0, ALU.mult, ALU.add)
                    last.then_inc(s_h, 1)

                def free_steps(eng, s, g, ring):
                    eng.wait_ge(s, i * NG + lowered(g, ring - 1, i))

                def finish(d):
                    dve.wait_ge(s_ysum, i * NG + NS * (d + 1))
                    for k in range(2):
                        last = dve.scalar_tensor_tensor(uu[:, d, k], uu[:, d, k], d_p[:, d, k:k + 1], ps_y[k][:, :],
                                                        ALU.mult, ALU.add)
                    then(last)
                    dve.tensor_tensor(sz[:, d], uu[:, d], sz[:, d], ALU.mult).then_inc(s_y, 1)

                def step(d, k, n, g):
                    dve.wait_ge(s_b_fill, i * NG + (g + 1))
                    free_steps(dve, s_h, g, 2)
                    dve.tensor_tensor(dBu[:, k % 2], du[:, d], ps_b[k % 2][:, :].unsqueeze(1).broadcast_to([P, 2, T]),
                                      ALU.mult).then_inc(s_dBu, 1)
                    if isinstance(n, int) and n == 0:
                        if d == 1:
                            scan(0, 3, g - 1)
                    else:
                        scan(d, (k - 1) % 4, g - 1)
                    if d == 1 and isinstance(n, int) and n == 3:
                        finish(0)

                n_steps(dve, step)
                scan(1, 3, NG - 1)
                finish(1)
                dve.wait_ge(s_o_fill, i + 1)
                dve.wait_ge(s_out, i * 16)
                dve.scalar_tensor_tensor(yo[:, :, :], ps_y[0][:, :].rearrange("p (c n) -> p c n", c=NC), 0.5,
                                         acc[:, :, :], ALU.mult, ALU.add).then_inc(s_yo, 1)
                assert done[0] == per, done

        @block.gpsimd
        def _(pool):
            pool.memset(xi[:, :, :, :], 0.0).then_inc(s_setup, 1)
            pool.memset(g_t[:, :, :], 1.0).then_inc(s_setup, 1)
            per = P_STEPS
            with pool.Fori(0, NB) as i:
                done = [0]

                def then(ins):
                    done[0] += 1
                    ins.then_inc(s_p, 1)
                    pool.wait_ge(s_p, i * per + done[0])

                for d in range(2):
                    G.wait_emptied(pool, i, "xd", d)
                    pool.wait_ge(s_ysum, i * NG)
                    alone(pool, s_pass)
                    then(pool.tensor_copy(bc[0:NS2, d], xd[0:NS2, d]))
                    then(pool.tensor_tensor(bc_r[:, d], xd[0:NS2, d], bc[0:NS2, d], ALU.subtract))
                    alone(pool, s_pass)
                    then(pool.tensor_copy(bc_m[:, d], bc_r[:, d]))
                    pool.tensor_tensor(bc_l[:, d], bc_r[:, d], bc_m[:, d], ALU.subtract).then_inc(s_lo, 1)

                def step(d, k, n, g):
                    pool.wait_ge(s_h, i * NG + (g + 1))
                    pool.wait_ge(s_c, i * NG + (g + 1))
                    pool.wait_ge(s_ysum, i * NG + lowered(g, RING - 1, i))
                    r = k % RING
                    pool.tensor_tensor(hc[:, r], h[:, r], c_n[:, r].unsqueeze(1).broadcast_to([P, 2, T]), ALU.mult)\
                        .then_inc(s_hc, 1)

                n_steps(pool, step)
                assert done[0] == per, done

        @block.scalar
        def _(act):
            act.preload_act_table_set("natural_log_exp_and_others")
            act.wait_ge(s_const, consts_in)
            act.activation(a_neg[:, :, :, :], a_log[:, :, :, :], ACT.Exp).then_inc(s_a, 1)
            act.wait_ge(s_a, 1)
            act.mul(a_neg[:, :, :, :], a_neg[:, :, :, :], -1.0).then_inc(s_a, 1)
            act.wait_ge(s_a, 2)
            act.wait_ge(s_setup, 2)
            with act.Fori(0, NB) as i:
                act.preload_act_table_set("natural_log_exp_and_others")
                act.wait_ge(s_var, i + 1)
                act.activation(lnv[:, :], var[:, :], ACT.Ln).then_inc(s_lnv, 1)
                act.wait_ge(s_lnv, i + 1)
                act.activation(rstd[:, :], lnv[:, :], ACT.Exp, scale=-0.5).then_inc(s_rstd, 1)
                G.wait_filled(act, i, "xnT")
                G.emptied(act.copy(xnT[:, :], G.bank("xnT")[:, :]), "xnT")
                act.wait_ge(s_gm, i + 1)
                act.activation(ge[:, :, :], gp[:, :, :], ACT.Exp).then_inc(s_ge, 1)
                for d in range(2):
                    for k in range(4):
                        G.wait_filled(act, i, "in", d, k)
                        if k < 2:
                            ins = act.copy(xi[:, d, k, KC - 1:KC - 1 + T], G.bank("in", d, k)[:, :])
                        else:
                            ins = act.activation(sz[:, d, k - 2], G.bank("in", d, k)[:, :], ACT.Silu)
                        G.emptied(ins, "in", d, k)

                def silu_u(d):
                    act.wait_ge(s_cv, i * 2 + d + 1)
                    act.activation(uu[:, d], cv[:, :, :], ACT.Silu).then_inc(s_u, 1)

                def silu_p1(e, order):
                    for k in range(2):
                        G.wait_filled(act, i, "p1", e, k)
                        last = (shared + list(range(NR)))[order - 1] if order else None
                        if order:
                            G.wait_emptied(act, i, "p2", last, k)
                        G.emptied(act.activation(s1[:, k], G.bank("p1", e, k)[:, :], ACT.Silu, bias=b1[:, e, k:k + 1]),
                                  "p1", e, k)

                silu_p1(shared[0], 0)
                silu_u(0)
                silu_p1(shared[1], 1)
                silu_u(1)
                G.wait_filled(act, i, "gT")
                G.emptied(act.copy(gT[:, :], G.bank("gT")[0:NX1, :]), "gT")
                for d in range(2):
                    G.wait_filled(act, i, "xd", d)
                    G.emptied(act.copy(xd[:, d], G.bank("xd", d)[0:NX, :]), "xd", d)
                for e in range(NR):
                    silu_p1(e, 2 + e)
                    if e in (3, 5):
                        d = (e - 3) // 2
                        act.wait_ge(s_lo, i * 2 + d + 1)
                        act.copy(bc[NS2:2 * NS2, d], bc_m[:, d])
                        act.copy(bc[2 * NS2:, d], bc_l[:, d]).then_inc(s_bc, 1)
                act.preload_act_table_set("natural_log_exp_and_others")
                for d in range(2):
                    act.wait_ge(s_delta, i * 2 + d)
                    for k in range(2):
                        G.wait_filled(act, i, "dl", d, k)
                        G.emptied(act.activation(dl[:, k], G.bank("dl", d, k)[:, :], ACT.Identity, bias=dt_b[:, d, k:k + 1]),
                                  "dl", d, k)
                    for k in range(2):
                        G.wait_emptied(act, i, "dl", d, k)
                    act.activation(sp_l[:, :, :], dl[:, :, :], ACT.Abs).then_inc(s_abs, 1)
                    act.wait_ge(s_abs, i * 2 + d + 1)
                    act.activation(sp_e[:, :, :], sp_l[:, :, :], ACT.Exp, scale=-1.0).then_inc(s_e, 1)
                    act.wait_ge(s_e, i * 2 + d + 1)
                    act.activation(sp_l[:, :, :], sp_e[:, :, :], ACT.Ln, bias=1.0).then_inc(s_l, 1)

                def step(d, k, n, g):
                    if isinstance(n, int) and n == 0:
                        act.wait_ge(s_delta, i * 2 + d + 1)
                    act.wait_ge(s_h, i * NG + lowered(g, RING - 1, i))
                    for b in range(2):
                        scale = a_neg[:, d, b, bass.ds(n, 1)] if not isinstance(n, int) else a_neg[:, d, b, n:n + 1]
                        last = act.activation(dA[:, k % RING, b], delta[:, d, b], ACT.Exp, scale=scale)
                    last.then_inc(s_dA, 1)
                    act.wait_ge(s_c_fill, i * NG + (g + 1))
                    act.wait_ge(s_hc, i * NG + lowered(g, RING - 1, i))
                    act.copy(c_n[:, k % RING], ps_c[:, :]).then_inc(s_c, 1)

                n_steps(act, step)

        @block.tensor
        def _(pe):
            pe.wait_ge(s_const, consts_in)
            pe.wait_ge(s_sel, 1)
            pe.wait_ge(s_setup, 2)
            with pe.Fori(0, NB) as i:
                pe.wait_ge(s_xn, i + 1)
                G.wait_free(pe, i, "xnT")
                for c in range(NC):
                    last = pe.transpose(G.bank("xnT")[:, P * c:P * c + P], xn[:, c], ident[:, :])
                G.filled(last, "xnT")
                G.wait_emptied(pe, i, "xnT")
                G.wait_free(pe, i, "gate")
                for c in range(NC):
                    last = pe.matmul(G.bank("gate")[:, NR * c:NR * c + NR], xnT[:, P * c:P * c + P], gate_w[:, :],
                                     start=True, stop=True)
                G.filled(last, "gate")
                for d in range(2):
                    for k in range(4):
                        G.wait_free(pe, i, "in", d, k)
                        G.filled(pe.matmul(G.bank("in", d, k)[:, :], in_w[:, d, P * k:P * k + P], xnT[:, :],
                                           start=True, stop=True), "in", d, k)

                def up(e):
                    for k in range(2):
                        for p, w in (("p1", w1), ("p2", w2)):
                            G.wait_free(pe, i, p, e, k)
                            G.filled(pe.matmul(G.bank(p, e, k)[:, :], w[:, e, P * k:P * k + P], xnT[:, :],
                                               start=True, stop=True), p, e, k)

                def down(e, order):
                    G.wait_free(pe, i, "out", e)
                    G.wait_emptied(pe, i, "p2", e, 1)
                    for c in range(NC):
                        for k in range(2):
                            last = pe.matmul(G.bank("out", e)[:, P * c:P * c + P], glu[:, order % 2, k, P * c:P * c + P],
                                             w3[:, e, k, :], start=(k == 0), stop=(k == 1))
                    G.filled(last, "out", e)

                def x_dbl(d):
                    pe.wait_ge(s_u, i * 2 + d + 1)
                    G.wait_free(pe, i, "xd", d)
                    for k in range(2):
                        last = pe.matmul(G.bank("xd", d)[0:NX, :], x_w[:, d, k, :], uu[:, d, k], start=(k == 0), stop=(k == 1))
                    G.filled(last, "xd", d)

                up(shared[0])
                up(shared[1])
                pe.wait_ge(s_gt, i + 1)
                G.wait_free(pe, i, "gT")
                for c in range(NC):
                    last = pe.transpose(G.bank("gT")[0:NX1, P * c:P * c + P], g_t[:, c], ident[:, :])
                G.filled(last, "gT")
                x_dbl(0)
                G.wait_free(pe, i, "out", "shared")
                G.wait_emptied(pe, i, "gT")
                G.wait_emptied(pe, i, "p2", shared[0], 1)
                G.wait_emptied(pe, i, "p2", shared[1], 1)
                for c in range(NC):
                    o = G.bank("out", "shared")[:, P * c:P * c + P]
                    pe.matmul(o, gT[:, P * c:P * c + P], b3[:, :], start=True, stop=False)
                    for order in range(2):
                        for k in range(2):
                            last = pe.matmul(o, glu[:, order, k, P * c:P * c + P], w3[:, shared[order], k, :],
                                             start=False, stop=(order == 1 and k == 1))
                G.filled(last, "out", "shared")
                x_dbl(1)
                for e in range(NR):
                    up(e)
                    if e:
                        down(e - 1, 1 + e)
                down(NR - 1, 1 + NR)
                for d in range(2):
                    G.wait_emptied(pe, i, "xd", d)
                    for k in range(2):
                        G.wait_free(pe, i, "dl", d, k)
                        alone(pe, s_pass)
                        G.filled(pe.matmul(G.bank("dl", d, k)[:, :], dt_w[NS2:NX, d, P * k:P * k + P], xd[NS2:NX, d],
                                           start=True, stop=True), "dl", d, k)

                def y_sum(d, k, g, first, last_n):
                    pe.wait_ge(s_hc, i * NG + (g + 1))
                    if first:
                        if d == 0:
                            pe.wait_ge(s_yo, i)
                        else:
                            pe.wait_ge(s_y, i * 2 + 1)
                    for b in range(2):
                        ins = pe.matmul(ps_y[b][:, :], ident[:, :], hc[:, k % RING, b], start=first, stop=last_n)
                    ins.then_inc(s_ysum, 1)

                def step(d, k, n, g):
                    pe.wait_ge(s_bc, i * 2 + d + 1)
                    pe.wait_ge(s_dBu, i * NG + lowered(g, 1, i))
                    row = (lambda r: sel[:, r, :]) if isinstance(n, int) else (lambda r: sel[:, bass.ds(r, 1), :])
                    pe.matmul(ps_b[k % 2][:, :], row(n), bc[:, d], start=True, stop=True).then_inc(s_b_fill, 1)
                    pe.wait_ge(s_c, i * NG + g)
                    pe.matmul(ps_c[:, :], row(n + NS), bc[:, d], start=True, stop=True).then_inc(s_c_fill, 1)
                    if not isinstance(n, int):
                        y_sum(d, (k - LAG) % 4, g - LAG, False, False)
                    elif n >= LAG:
                        y_sum(d, k - LAG, g - LAG, n == LAG, False)
                    elif d == 1:
                        y_sum(0, (k - LAG) % 4, g - LAG, False, n == LAG - 1)

                n_steps(pe, step)
                for k in range(4 - LAG, 4):
                    y_sum(1, k, NG - 4 + k, False, k == 3)
                pe.wait_ge(s_y, i * 2 + 2)
                for c in range(NC):
                    for d in range(2):
                        for k in range(2):
                            last = pe.matmul(ps_y[0][:, P * c:P * c + P], sz[:, d, k, P * c:P * c + P], out_w[:, d, k, :],
                                             start=(d == 0 and k == 0), stop=(d == 1 and k == 1))
                last.then_inc(s_o_fill, 1)


def build(nc, a, out):
    scr = {
        "xn": nc.dram_tensor("scratch_xn", (NB * T, E0), F32).ap(),
        "lg": nc.dram_tensor("scratch_lg", (NB * NE, T), F32).ap(),
        "x1": nc.dram_tensor("scratch_x1", (NB * T, E0), F32).ap(),
    }
    attention_phase(nc, a, scr)
    expert_phase(nc, a, scr)
    layer1_phase(nc, a, scr, out)


def kernel(**inputs):
    import concourse.bacc as _bacc
    from concourse.bass_utils import run_bass_kernel_spmd as _run

    arrays = {k: np.ascontiguousarray(v) for k, v in inputs.items()}
    arrays.update(layouts(arrays))
    arrays.update(constants())
    unused = {f"L1_attn_{k}_{s}" for s in "fb"
              for k in ("inW", "convW", "convB", "xpW", "dtW", "dtB", "Alog", "Dp", "outW")}
    unused |= {"L1_ffn_rb1", "L1_ffn_rb2", "L1_ffn_sb1", "L1_ffn_sb2"}
    arrays = {k: v for k, v in arrays.items() if k not in unused}
    nc = _bacc.Bacc("TRN2", target_bir_lowering=False, num_devices=1)
    a = {k: nc.dram_tensor("in_" + k, v.shape, mybir.dt.from_np(v.dtype), kind="ExternalInput").ap()
         for k, v in arrays.items()}
    out = nc.dram_tensor("out", (NB, T, E0), F32, kind="ExternalOutput").ap()
    build(nc, a, out)
    r = _run(nc, [{"in_" + k: v for k, v in arrays.items()}], core_ids=[0])
    return r.results[0]["out"]
```

```python
from contextlib import ExitStack

import numpy as np
import concourse.bass as bass
from concourse import mybir

F32 = mybir.dt.float32
BF16 = mybir.dt.bfloat16
U32 = mybir.dt.uint32
ALU = mybir.AluOpType
ACT = mybir.ActivationFunctionType
AX = mybir.AxisListType

P = 128
NB, T, E0 = 8, 512, 128
NC = T // P
NH = 16
HD = E0 // NH
BW = 32
KW = 2 * BW
NQ = T // BW
XP = 3 * BW
NE, TOPK = 16, 32
NS, DI, KC, NX = 16, 256, 4, 40
NS2 = 2 * NS
NG = 2 * NS
RING = 4
LAG = 3
NR, NX1, DH = 8, 10, 256
V_BEFORE, V_STEPS = 17, 25
P_BEFORE, P_STEPS = 3, 6
SETUP = 6
PAIRED = (1, 3, 7, 9, 13, 15)
LN_EPS = 1e-5
RMS_EPS = float(np.finfo(np.float32).eps)


def constants():
    q = np.arange(P) % BW
    k = np.arange(KW)
    seen = (k[None] > q[:, None]) & (k[None] <= q[:, None] + BW)
    no_past = seen & ~((np.arange(P) < BW)[:, None] & (k < BW)[None])
    band = np.where(np.stack([seen, no_past], 1), 0.0, MASKED).astype(np.float32)
    head = (np.arange(P) // HD) % 4
    return {
        "c_ident": np.eye(P, dtype=np.float32),
        "c_band": band,
        "c_row0": (np.arange(P, dtype=np.float32) // NE * T)[:, None],
        "c_sel": np.tile(np.eye(NS2, dtype=np.float32), (3, 1)),
        "c_iota": np.tile(np.arange(NR, dtype=np.float32), (P, 1)),
        "c_head_of_4": (head[:, None] == np.arange(4)[None]).astype(np.float32),
    }


MASKED = -1e30


def layouts(a):
    blocks = lambda x: np.ascontiguousarray(x.reshape(2, P, -1).transpose(1, 0, 2))
    t = {}
    for s in "fb":
        w = {k: a[f"L1_attn_{k}_{s}"] for k in ("inW", "convW", "convB", "xpW", "dtW", "dtB", "Alog", "Dp", "outW")}
        t["t_in_w_" + s] = np.ascontiguousarray(w["inW"].T)
        t["t_conv_w_" + s] = blocks(w["convW"][:, 0])
        t["t_conv_b_" + s] = blocks(w["convB"])[:, :, 0]
        bcd = np.concatenate([w["xpW"][NX - NS2:], w["xpW"][:NX - NS2]])
        t["t_x_w_" + s] = blocks(bcd.T)
        t["t_dt_w_" + s] = np.ascontiguousarray(w["dtW"].T)
        t["t_dt_b_" + s] = blocks(w["dtB"])[:, :, 0]
        t["t_a_log_" + s] = blocks(w["Alog"])
        t["t_d_p_" + s] = blocks(w["Dp"])[:, :, 0]
        t["t_out_w_" + s] = blocks(w["outW"].T)
    for n in (1, 2):
        b = np.concatenate([a[f"L1_ffn_rb{n}"], a[f"L1_ffn_sb{n}"]])
        t[f"t_b{n}"] = b.reshape(NX1, 2, P).transpose(2, 0, 1)
    return {k: np.ascontiguousarray(v) for k, v in t.items()}


def summed(n):
    return 2 if n in PAIRED else 0 if n + 1 in PAIRED else 1


def alone(eng, s_pass):
    eng.sem_inc(s_pass, 1)


class Banks:

    def __init__(self, sem, name, tiles, uses, before=()):
        n = len(tiles)
        assert len(set(uses)) == len(uses)
        self.tiles = tiles
        self.fill = [sem(f"{name}_fill{k}") for k in range(n)]
        self.empty = [sem(f"{name}_empty{k}") for k in range(n)]
        self.at, self.base, self.per = {}, [0] * n, [0] * n
        for m, key in enumerate(before):
            self.at[("before", *key)] = (m % n, self.base[m % n])
            self.base[m % n] += 1
        for m, key in enumerate(uses):
            k = (m + len(before)) % n
            self.at[key] = (k, self.per[k])
            self.per[k] += 1

    def bank(self, *key):
        return self.tiles[self.at[key][0]]

    def count(self, i, key):
        k, n = self.at[key]
        return n if key[0] == "before" else i * self.per[k] + (self.base[k] + n)

    def wait_filled(self, eng, i, *key):
        eng.wait_ge(self.fill[self.at[key][0]], self.count(i, key) + 2)

    def wait_free(self, eng, i, *key):
        eng.wait_ge(self.empty[self.at[key][0]], self.count(i, key) + 1)

    def wait_emptied(self, eng, i, *key):
        eng.wait_ge(self.empty[self.at[key][0]], self.count(i, key) + 2)

    def filled(self, ins, *key):
        ins.then_inc(self.fill[self.at[key][0]], 1)

    def emptied(self, ins, *key):
        ins.then_inc(self.empty[self.at[key][0]], 1)


def attention_phase(nc, a, scr):
    U = 2
    ctx = ExitStack()
    with ctx:
        def sb(name, shape, dt=F32):
            return ctx.enter_context(nc.sbuf_tensor(name, shape, dt))

        semaphores = []

        def sem(name):
            semaphores.append(ctx.enter_context(nc.semaphore(name)))
            return semaphores[-1]

        ident = sb("a_ident", [P, P])
        w_qk = sb("a_w_qk", [P, 2 * E0])
        w_v = sb("a_w_v", [P, E0])
        w_o = sb("a_w_o", [P, E0])
        w_g = sb("a_w_g", [P, NE])
        b_g = sb("a_b_g", [NE, 1])
        b_qk = sb("a_b_qk", [P, 2 * E0])
        b_v = sb("a_b_v", [P, E0])
        b_o = sb("a_b_o", [P, E0])
        qn_b = sb("a_qn_b", [P, HD])
        kn_b = sb("a_kn_b", [P, HD])
        qk_w = sb("a_qk_w", [P, HD])
        band = sb("a_band", [P, 2, KW])
        head_of_4 = sb("a_head_of_4", [P, 4])
        xt = sb("a_xt", [P, U, NC, E0])
        xb = sb("a_xb", [P, U, NC, E0])
        xn = sb("a_xn", [P, U, NC, E0])
        stats = sb("a_stats", [P, U, NC, 6])
        mv = sb("a_mv", [P, U, NC, 2])
        var = sb("a_var", [P, U, NC])
        lnv = sb("a_lnv", [P, U, NC])
        rstd = sb("a_rstd", [P, U, NC])
        xnT = sb("a_xnT", [P, U, XP + T])
        lg = sb("a_lg", [NE, U, T])
        qk = sb("a_qk", [P, U, NC, 2 * E0])
        sq = sb("a_sq", [P, U, NC, 2 * E0])
        ms = sb("a_ms", [P, U, NC * 2 * NH])
        mse = sb("a_mse", [P, U, NC * 2 * NH])
        lms = sb("a_lms", [P, U, NC * 2 * NH])
        rs = sb("a_rs", [P, U, NC * 2 * NH])
        qn = sb("a_qn", [P, U, NC, 2 * E0])
        qT = sb("a_qT", [P, U, T])
        kblk = sb("a_kblk", [P, U, 4, BW + T])
        prob = sb("a_prob", [P, U, 2, NH, KW])
        mx = sb("a_mx", [P, U, 2 * NH])
        pT = sb("a_pT", [P, 2, 4, P])
        vblk = sb("a_vblk", [P, U, NQ, NH // 2, 2 * (HD + 1)])
        rc = sb("a_rc", [P, U, 2, NH])
        att = sb("a_att", [P, U, NC, E0])
        attT = sb("a_attT", [P, U, T])
        x1 = sb("a_x1", [P, U, NC, E0])

        ps_s = ctx.enter_context(nc.psum_tensor("a_ps_s", [P, 4, 512], F32))
        ps_g = [ctx.enter_context(nc.psum_tensor(f"a_ps_g{n}", [P, 512], F32)) for n in range(2)]
        ps_h = [ctx.enter_context(nc.psum_tensor(f"a_ps_h{n}", [P, 512], F32)) for n in range(2)]

        order = [(0, 0), (1, 0), (0, 1), (1, 1)]
        head = [("xnT", u) for u in range(U)] + [("lg", u) for u in range(U)]
        turned = [[("qT", u), ("kT", u)] for u in range(U)]
        quarters = [[("pT", u, cp, k) for k in range(4)] for u, cp in order]
        g_uses = quarters[0] + quarters[1] + head + quarters[2] + turned[0] + quarters[3] + turned[1]
        g_uses += [("attT", u) for u in range(U)] + [("wo", u) for u in range(U)]
        h_uses = [("v", u, n) for u in range(U) for n in range(5)] + [("pv", u, cp) for u, cp in order]
        G = Banks(sem, "a_g", ps_g, g_uses, head + turned[0] + turned[1])
        H = Banks(sem, "a_h", ps_h, h_uses)

        def pool_of(key):
            return H if key[0] in ("v", "pv") else G

        def bank(*key):
            return pool_of(key).bank(*key)

        def fill_wait(eng, i, *key):
            pool_of(key).wait_filled(eng, i, *key)

        def free_wait(eng, i, *key):
            pool_of(key).wait_free(eng, i, *key)

        def evac_wait(eng, i, *key):
            pool_of(key).wait_emptied(eng, i, *key)

        def filled(ins, *key):
            pool_of(key).filled(ins, *key)

        def emptied(ins, *key):
            pool_of(key).emptied(ins, *key)

        s_pass = sem("a_pass")
        s_const = sem("a_const")
        s_head_const = sem("a_head_const")
        s_zero = sem("a_zero")
        s_qkw = sem("a_qkw")
        s_x = [sem(f"a_x{u}") for u in range(U)]
        s_xn_out = [sem(f"a_xn_out{u}") for u in range(U)]
        s_lg_out = [sem(f"a_lg_out{u}") for u in range(U)]
        s_x1_out = [sem(f"a_x1_out{u}") for u in range(U)]
        s_stats = sem("a_stats_ready")
        s_mv = sem("a_mv_ready")
        s_var = sem("a_var_ready")
        s_ln = sem("a_ln_ready")
        s_rstd = sem("a_rstd_ready")
        s_xn = sem("a_xn_ready")
        s_xb = sem("a_xb_ready")
        s_qk_fill = sem("a_qk_filled")
        s_qk = sem("a_qk_ready")
        s_sq = sem("a_sq_ready")
        s_ms = sem("a_ms_ready")
        s_mse = sem("a_mse_ready")
        s_lms = sem("a_lms_ready")
        s_rs = sem("a_rs_ready")
        s_qn0 = sem("a_qn_scaled")
        s_qn = sem("a_qn_ready")
        s_sc = sem("a_scores_filled")
        s_masked = sem("a_scores_masked")
        s_mx = sem("a_max_ready")
        s_sub = sem("a_max_subtracted")
        s_p = sem("a_prob_ready")
        s_pv = sem("a_pT_used")
        s_rc = sem("a_rc_ready")
        s_att = sem("a_att_ready")

        n_iter = NB // U
        x_v = a["L0_attn_x"].rearrange("b (c p) e -> b p c e", p=P)
        xn_v = scr["xn"].rearrange("(b c p) e -> b p c e", b=NB, p=P)
        x1_v = scr["x1"].rearrange("(b c p) e -> b p c e", b=NB, p=P)
        lg_v = scr["lg"].rearrange("(b e) t -> b e t", b=NB)
        head_loads = [
            (ident[:, :], a["c_ident"]), (w_g[:, :], a["L0_ffn_Wg"]), (b_g[:, :], a["L0_ffn_bg"].unsqueeze(1)),
            (w_qk[:, 0:E0], a["L0_attn_wq"]), (w_qk[:, E0:], a["L0_attn_wk"]),
        ]
        loads = [
            (band[:, :, :], a["c_band"]), (head_of_4[:, :], a["c_head_of_4"]),
            (w_v[:, :], a["L0_attn_wv"]), (w_o[:, :], a["L0_attn_wo"]),
            (b_qk[:, 0:E0], a["L0_attn_bq"].partition_broadcast(P)),
            (b_qk[:, E0:], a["L0_attn_bk"].partition_broadcast(P)),
            (b_v[:, :], a["L0_attn_bv"].partition_broadcast(P)),
            (b_o[:, :], a["L0_attn_bo"].partition_broadcast(P)),
            (qn_b[:, :], a["L0_attn_qn_w"].partition_broadcast(P)),
            (kn_b[:, :], a["L0_attn_kn_w"].partition_broadcast(P)),
        ]
        consts_in = 16 * len(loads)
        head_consts_in = 16 * len(head_loads)
        block = ctx.enter_context(nc.Block())

        @block.sync
        def _(sp):
            def store_head(pre, i, j, pair):
                for u in range(U):
                    sp.wait_ge(s_xn, j * U + (u + 2))
                    sp.dma_start(xn_v[pair * U + u], xn[:, u]).then_inc(s_xn_out[u], 16)
                for u in range(U):
                    evac_wait(sp, i, *pre, "lg", u)
                    sp.dma_start(lg_v[pair * U + u], lg[:, u]).then_inc(s_lg_out[u], 16)

            for u in range(U):
                sp.dma_start(xt[:, u], x_v[u]).then_inc(s_x[u], 16)
            for dst, src in head_loads:
                sp.dma_start(dst, src).then_inc(s_head_const, 16)
            for dst, src in loads:
                sp.dma_start(dst, src).then_inc(s_const, 16)
            store_head(("before",), 0, 0, 0)
            with sp.Fori(0, n_iter) as i:
                ahead = (i + 1) % n_iter
                for u in range(U):
                    sp.wait_ge(s_xb, i * U + u + 2)
                    sp.dma_start(xt[:, u], x_v[ahead * U + u]).then_inc(s_x[u], 16)
                store_head((), i, i + 1, ahead)
                for u in range(U):
                    evac_wait(sp, i, "wo", u)
                    sp.dma_start(x1_v[i * U + u], x1[:, u]).then_inc(s_x1_out[u], 16)
            for u in range(U):
                sp.wait_ge(s_x[u], 16 * (n_iter + 1) + 1)
                sp.wait_ge(s_xn_out[u], 16 * (n_iter + 1) + 1)
                sp.wait_ge(s_lg_out[u], 16 * (n_iter + 1) + 1)
                sp.wait_ge(s_x1_out[u], 16 * n_iter + 1)

        @block.gpsimd
        def _(pool):
            for s in semaphores:
                pool.sem_inc(s, 1)
            pool.memset(xnT[:, :, 0:XP], 0.0).then_inc(s_zero, 1)
            pool.memset(kblk[:, :, :, 0:BW], 0.0).then_inc(s_zero, 1)
            pool.memset(vblk[:, :, :, :, :], 0.0).then_inc(s_zero, 1)
            pool.wait_ge(s_zero, 4)
            for u in range(U):
                pool.memset(vblk[0:64, u, :, :, HD:HD + 1], 1.0).then_inc(s_zero, 1)
                pool.memset(vblk[64:P, u, :, :, 2 * HD + 1:], 1.0).then_inc(s_zero, 1)
        zeroed = 3 + 2 * U

        @block.scalar
        def _(act):
            act.preload_act_table_set("natural_log_exp_and_others")

            def rstds(j):
                for u in range(U):
                    n = j * U + (u + 1)
                    act.wait_ge(s_var, n + 1)
                    act.activation(lnv[:, u], var[:, u], ACT.Ln).then_inc(s_ln, 1)
                    act.wait_ge(s_ln, n + 1)
                    act.activation(rstd[:, u], lnv[:, u], ACT.Exp, scale=-0.5).then_inc(s_rstd, 1)

            def head_out(pre, i, j):
                for u in range(U):
                    fill_wait(act, i, *pre, "xnT", u)
                    emptied(act.copy(xnT[:, u, XP:], bank(*pre, "xnT", u)[:, :]), *pre, "xnT", u)
                for u in range(U):
                    fill_wait(act, i, *pre, "lg", u)
                    act.wait_ge(s_lg_out[u], j * 16 + 1)
                    emptied(act.activation(lg[:, u], bank(*pre, "lg", u)[0:NE, :], ACT.Identity, bias=b_g[:, :]),
                            *pre, "lg", u)

            def squares(j):
                for u in range(U):
                    act.wait_ge(s_qk, j * U + (u + 2))
                    act.activation(sq[:, u], qk[:, u], ACT.Square).then_inc(s_sq, 1)

            def rms(j):
                for u in range(U):
                    n = j * U + (u + 1)
                    act.wait_ge(s_mse, n + 1)
                    act.activation(lms[:, u], mse[:, u], ACT.Ln).then_inc(s_lms, 1)
                    act.wait_ge(s_lms, n + 1)
                    act.activation(rs[:, u], lms[:, u], ACT.Exp, scale=-0.5).then_inc(s_rs, 1)

            def turned_out(pre, i, u):
                fill_wait(act, i, *pre, "qT", u)
                emptied(act.copy(qT[:, u], bank(*pre, "qT", u)[:, :]), *pre, "qT", u)
                fill_wait(act, i, *pre, "kT", u)
                for h in range(4):
                    last = act.activation(kblk[:, u, h, BW:], bank(*pre, "kT", u)[:, :], ACT.Copy,
                                          scale=head_of_4[:, h:h + 1])
                emptied(last, *pre, "kT", u)

            rstds(0)
            act.wait_ge(s_head_const, head_consts_in + 1)
            act.wait_ge(s_zero, zeroed + 1)
            head_out(("before",), 0, 0)
            act.wait_ge(s_const, consts_in + 1)
            squares(0)
            rms(0)
            for u in range(U):
                turned_out(("before",), 0, u)
            with act.Fori(0, n_iter) as i:
                def v_out(u):
                    for n in range(5):
                        fill_wait(act, i, "v", u, n)
                        for hh in range(2):
                            q = slice(64 * hh, 64 * hh + 64)
                            w0 = 2 if n == 0 and hh == 0 else 0
                            w1 = 2 if n == 4 else 4
                            if n == 4 and hh == 1:
                                continue
                            src = bank("v", u, n)[q, :].rearrange("p (w m h d) -> p w m h d", w=4, m=NH // 2, h=2)
                            to = 4 * n - 2 + 2 * hh
                            last = act.copy(vblk[q, u, to + w0:to + w1, :, hh * (HD + 1):hh * (HD + 1) + HD],
                                            src[:, w0:w1, :, hh])
                        emptied(last, "v", u, n)

                def exp(m):
                    u, cp = order[m]
                    act.wait_ge(s_sub, i * 4 + m + 2)
                    act.activation(prob[:, u], prob[:, u], ACT.Exp).then_inc(s_p, 1)

                v_out(0)
                exp(0)
                v_out(1)
                for m, (u, cp) in enumerate(order):
                    if m < 3:
                        exp(m + 1)
                    if m == 0:
                        rstds(i + 1)
                    for k in range(4):
                        fill_wait(act, i, "pT", u, cp, k)
                        if k != 1:
                            act.wait_ge(s_pv, i * 12 + 3 * m + max(k - 1, 0) + 1)
                        elif m:
                            fill_wait(act, i, "pv", *order[m - 1])
                        else:
                            act.wait_ge(H.fill[H.at[("pv", *order[3])][0]], i * H.per[0] + 1)
                        emptied(act.copy(pT[:, k % 2], bank("pT", u, cp, k)[:, :]
                                         .rearrange("p (h q) -> p h q", h=4)), "pT", u, cp, k)
                        if m == 2 and k == 0:
                            squares(i + 1)
                        if m == 2 and k == 2:
                            rms(i + 1)
                    if m == 1:
                        head_out((), i, i + 1)
                    if m >= 2:
                        turned_out((), i, m - 2)
                for u in range(U):
                    fill_wait(act, i, "attT", u)
                    emptied(act.copy(attT[:, u], bank("attT", u)[:, :]), "attT", u)

        @block.vector
        def _(dve):

            def variances(j):
                for u in range(U):
                    dve.wait_ge(s_x[u], j * 16 + 16 + 1)
                    for c in range(NC):
                        last = dve.bn_stats(stats[:, u, c], xt[:, u, c])
                    last.then_inc(s_stats, 1)
                    dve.wait_ge(s_stats, j * U + (u + 2))
                    alone(dve, s_pass)
                    for c in range(NC):
                        last = dve.bn_aggr(mv[:, u, c], stats[:, u, c])
                    last.then_inc(s_mv, 1)
                    dve.wait_ge(s_mv, j * U + (u + 2))
                    dve.tensor_scalar(var[:, u], mv[:, u, :, 1], LN_EPS, None, ALU.add).then_inc(s_var, 1)

            def norms(j):
                for u in range(U):
                    dve.wait_ge(s_rstd, j * U + (u + 2))
                    dve.wait_ge(s_xn_out[u], j * 16 + 1)
                    for c in range(NC):
                        last = dve.tensor_scalar(xn[:, u, c], xt[:, u, c], mv[:, u, c, 0:1], rstd[:, u, c:c + 1],
                                                 ALU.subtract, ALU.mult)
                    last.then_inc(s_xn, 1)

            def mean_squares(j):
                for u in range(U):
                    dve.wait_ge(s_qk_fill, j * U + (u + 2))
                    bias = b_qk[:, :].unsqueeze(1).broadcast_to([P, 2, 2 * E0])
                    for h in range(2):
                        last = dve.tensor_tensor(qk[:, u, 2 * h:2 * h + 2],
                                                 ps_s[:, 2 * u + h].rearrange("p (c n) -> p c n", c=2), bias, ALU.add)
                    last.then_inc(s_qk, 1)
                for u in range(U):
                    dve.wait_ge(s_sq, j * U + (u + 2))
                    dve.tensor_reduce(ms[:, u], sq[:, u].rearrange("p c (h d) -> p (c h) d", d=HD), AX.X, ALU.add)\
                       .then_inc(s_ms, 1)
                    dve.wait_ge(s_ms, j * U + (u + 2))
                    dve.tensor_scalar(mse[:, u], ms[:, u], 1.0 / HD, RMS_EPS, ALU.mult, ALU.add).then_inc(s_mse, 1)

            def qk_norms(j):
                for u in range(U):
                    dve.wait_ge(s_rs, j * U + (u + 2))
                    dve.tensor_tensor(qn[:, u].rearrange("p c (h d) -> p (c h) d", d=HD),
                                      qk[:, u].rearrange("p c (h d) -> p (c h) d", d=HD),
                                      rs[:, u].unsqueeze(2).broadcast_to([P, NC * 2 * NH, HD]), ALU.mult)\
                       .then_inc(s_qn0, 1)
                    dve.wait_ge(s_qn0, j * U + (u + 2))
                    q = qn[:, u, :, 0:E0].rearrange("p c (h d) -> p c h d", d=HD)
                    dve.tensor_tensor(q, q, qk_w[:, :].unsqueeze(1).unsqueeze(1).broadcast_to([P, NC, NH, HD]),
                                      ALU.mult).then_inc(s_qn, 1)

            dve.wait_ge(s_zero, 2)
            variances(0)
            norms(0)
            dve.wait_ge(s_const, consts_in + 1)
            dve.wait_ge(s_zero, zeroed + 1)
            dve.scalar_tensor_tensor(qk_w[:, :], qn_b[:, :], HD ** -0.5, kn_b[:, :], ALU.mult, ALU.mult)\
               .then_inc(s_qkw, 1)
            dve.wait_ge(s_qkw, 2)
            mean_squares(0)
            qk_norms(0)
            with dve.Fori(0, n_iter) as i:
                for u in range(U):
                    free_wait(dve, i, "pT", *order[0], u)
                    dve.tensor_tensor(xb[:, u], xt[:, u], b_o[:, :].unsqueeze(1).broadcast_to([P, NC, E0]),
                                      ALU.add).then_inc(s_xb, 1)
                def softmax(m):
                    u, cp = order[m]
                    n = i * 4 + m + 1
                    dve.wait_ge(s_sc, n + 1)
                    if cp == 1:
                        fill_wait(dve, i, "pT", u, 0, 3)
                    for cc in range(2):
                        first = 1 if cp == 0 and cc == 0 else 0
                        mask = band[:, first].unsqueeze(1).unsqueeze(1).broadcast_to([P, 4, 4, KW])
                        last = dve.tensor_tensor(
                            prob[:, u, cc].rearrange("p (g h) k -> p g h k", g=4),
                            ps_s[:, :, 256 * cc:256 * cc + 256].rearrange("p g (h k) -> p g h k", h=4), mask, ALU.add)
                    last.then_inc(s_masked, 1)
                    dve.wait_ge(s_masked, n + 1)
                    flat = prob[:, u].rearrange("p c h k -> p (c h) k")
                    dve.tensor_reduce(mx[:, u], flat, AX.X, ALU.max).then_inc(s_mx, 1)
                    dve.wait_ge(s_mx, n + 1)
                    dve.tensor_tensor(flat, flat, mx[:, u].unsqueeze(2).broadcast_to([P, 2 * NH, KW]),
                                      ALU.subtract).then_inc(s_sub, 1)

                def normalise(m):
                    u, cp = order[m]
                    fill_wait(dve, i, "pv", u, cp)
                    o = bank("pv", u, cp)[:, 0:2 * NH * (HD + 1)].rearrange("p (c h d) -> p c h d", c=2, h=NH)
                    dve.reciprocal(rc[:, u], o[:, :, :, HD]).then_inc(s_rc, 1)
                    dve.wait_ge(s_rc, i * 4 + m + 2)
                    to = att[:, u, 2 * cp:2 * cp + 2]
                    emptied(dve.tensor_tensor(to.rearrange("p c (h d) -> p c h d", d=HD), o[:, :, :, 0:HD],
                                              rc[:, u].unsqueeze(3).broadcast_to([P, 2, NH, HD]), ALU.mult), "pv", u, cp)
                    evac_wait(dve, i, "pv", u, cp)
                    dve.tensor_tensor(to, to, b_v[:, :].unsqueeze(1).broadcast_to([P, 2, E0]), ALU.add)\
                       .then_inc(s_att, 1)

                softmax(0)
                softmax(1)
                variances(i + 1)
                norms(i + 1)
                for m in range(4):
                    if m + 2 < 4:
                        softmax(m + 2)
                    if m == 2:
                        mean_squares(i + 1)
                        qk_norms(i + 1)
                    normalise(m)
                for u in range(U):
                    fill_wait(dve, i, "wo", u)
                    dve.wait_ge(s_x1_out[u], i * 16 + 1)
                    dve.wait_ge(s_xb, i * U + U + 1)
                    last = dve.tensor_tensor(x1[:, u], bank("wo", u)[:, :].rearrange("p (c n) -> p c n", c=NC),
                                             xb[:, u], ALU.add)
                    emptied(last, "wo", u)

        @block.tensor
        def _(pe):
            pe.wait_ge(s_head_const, head_consts_in + 1)
            pe.wait_ge(s_zero, zeroed + 1)

            def head_products(pre, i, j):
                for u in range(U):
                    pe.wait_ge(s_xn, j * U + (u + 2))
                    free_wait(pe, i, *pre, "xnT", u)
                    for c in range(NC):
                        last = pe.transpose(bank(*pre, "xnT", u)[:, P * c:P * c + P], xn[:, u, c], ident[:, :])
                    filled(last, *pre, "xnT", u)
                for u in range(U):
                    evac_wait(pe, i, *pre, "xnT", u)
                    free_wait(pe, i, *pre, "lg", u)
                    filled(pe.matmul(bank(*pre, "lg", u)[0:NE, :], w_g[:, :], xnT[:, u, XP:], start=True, stop=True),
                           *pre, "lg", u)
                if not pre:
                    pe.wait_ge(s_masked, i * 4 + 5)
                for u in range(U):
                    for c in range(NC):
                        out = ps_s[:, 2 * u + c // 2, 256 * (c % 2):256 * (c % 2) + 256]
                        last = pe.matmul(out, xnT[:, u, XP + P * c:XP + P * c + P], w_qk[:, :], start=True, stop=True)
                    last.then_inc(s_qk_fill, 1)

            def turn_qk(pre, i, j, u):
                pe.wait_ge(s_qn, j * U + (u + 2))
                for name, off in (("qT", 0), ("kT", E0)):
                    free_wait(pe, i, *pre, name, u)
                    for c in range(NC):
                        last = pe.transpose(bank(*pre, name, u)[:, P * c:P * c + P], qn[:, u, c, off:off + E0],
                                            ident[:, :])
                    filled(last, *pre, name, u)

            head_products(("before",), 0, 0)
            for u in range(U):
                turn_qk(("before",), 0, 0, u)
            pe.wait_ge(s_const, consts_in + 1)
            with pe.Fori(0, n_iter) as i:
                def v_products(u):
                    for n in range(5):
                        free_wait(pe, i, "v", u, n)
                        for w in range(2 if n == 4 else 4):
                            t0 = XP - BW + BW * (4 * n - 2 + w)
                            keys = KW if n == 4 else 2 * KW
                            last = pe.matmul(bank("v", u, n)[0:keys, P * w:P * w + P], xnT[:, u, t0:t0 + keys],
                                             w_v[:, :], start=True, stop=True)
                        filled(last, "v", u, n)

                def scores(m):
                    u, cp = order[m]
                    if m == 0:
                        pe.wait_ge(s_qk, i * U + U + 1)
                        free_wait(pe, i, "pT", *order[0], 0)
                        free_wait(pe, i, "pT", *order[0], 1)
                    else:
                        pe.wait_ge(s_masked, i * 4 + m + 1)
                    alone(pe, s_pass)
                    for cc in range(2):
                        for j in range(4):
                            t0 = P * (2 * cp + cc) + BW * j
                            for g in range(4):
                                q = slice(32 * g, 32 * g + 32)
                                last = pe.matmul(ps_s[32 * j:32 * j + 32, g, 256 * cc:256 * cc + 256],
                                                 qT[q, u, t0:t0 + BW], kblk[q, u, :, t0:t0 + KW],
                                                 start=True, stop=True)
                    last.then_inc(s_sc, 1)

                def turn(m, k):
                    u, cp = order[m]
                    free_wait(pe, i, "pT", u, cp, k)
                    pe.wait_ge(s_p, i * 4 + m + 2)
                    for n in range(4):
                        h = 8 * (k % 2) + 2 * n
                        last = pe.transpose(bank("pT", u, cp, k)[:, P * n:P * n + P],
                                            prob[:, u, k // 2, h:h + 2].rearrange("p h k -> p (h k)"), ident[:, :])
                    filled(last, "pT", u, cp, k)

                def p_v(m, k):
                    u, cp = order[m]
                    evac_wait(pe, i, "pT", u, cp, k)
                    if k == 0:
                        free_wait(pe, i, "pv", u, cp)
                    for n in range(4):
                        pair = 4 * (k % 2) + n
                        col = (k // 2) * NH * (HD + 1) + pair * 2 * (HD + 1)
                        for j in range(4):
                            w = 4 * (2 * cp + k // 2) + j
                            last = pe.matmul(bank("pv", u, cp)[32 * j:32 * j + 32, col:col + 2 * (HD + 1)],
                                             pT[:, k % 2, n, 32 * j:32 * j + 32], vblk[:, u, w, pair, :],
                                             start=True, stop=True)
                    if k < 3:
                        last.then_inc(s_pv, 1)
                    else:
                        filled(last, "pv", u, cp)

                scores(0)
                v_products(0)
                scores(1)
                v_products(1)
                for m in range(4):
                    if m + 2 < 4:
                        scores(m + 2)
                    for k in range(4):
                        turn(m, k)
                        if k:
                            p_v(m, k - 1)
                    p_v(m, 3)
                    if m == 1:
                        head_products((), i, i + 1)
                    if m >= 2:
                        turn_qk((), i, i + 1, m - 2)
                for u in range(U):
                    free_wait(pe, i, "attT", u)
                    pe.wait_ge(s_att, i * 4 + u + 4)
                    for c in range(NC):
                        last = pe.transpose(bank("attT", u)[:, P * c:P * c + P], att[:, u, c], ident[:, :])
                    filled(last, "attT", u)
                for u in range(U):
                    free_wait(pe, i, "wo", u)
                    evac_wait(pe, i, "attT", u)
                    for c in range(NC):
                        last = pe.matmul(bank("wo", u)[:, P * c:P * c + P], attT[:, u, P * c:P * c + P], w_o[:, :],
                                         start=True, stop=True)
                    filled(last, "wo", u)


def expert_phase(nc, a, scr, ahead):
    U = 4
    ctx = ExitStack()
    with ctx:
        def sb(name, shape, dt=F32):
            return ctx.enter_context(nc.sbuf_tensor(name, shape, dt))

        semaphores = []

        def sem(name, start=1):
            semaphores.append((ctx.enter_context(nc.semaphore(name)), start))
            return semaphores[-1][0]

        def wait_expert(eng, s, e):
            eng.wait_ge(s, e + (U + 1))

        def sem_from_0(name):
            return ctx.enter_context(nc.semaphore(name))

        ident = sb("b_ident", [P, P])
        row0 = sb("b_row0", [P, 1])
        bias = sb("b_bias", [P, 3, NE])
        lg = sb("b_lg", [P, T])
        ex = sb("b_ex", [P, T])
        pr = sb("b_pr", [P, 2, T])
        mx = sb("b_mx", [P, 1])
        nmx = sb("b_nmx", [P, 1])
        ssum = sb("b_ssum", [P, 1])
        rsum = sb("b_rsum", [P, 1])
        vals = sb("b_vals", [P, TOPK])
        idx = sb("b_idx", [P, TOPK], U32)
        rowf = sb("b_rowf", [P, TOPK])
        row_at = sb("b_row_at", [P, NE, 2], U32)
        val_at = sb("b_val_at", [P, NE, 2])
        row_in = sb("b_row_in", [P, U, 2], U32)
        row_now = sb("b_row_now", [P, U, 2], U32)
        val_now = sb("b_val_now", [P, U, 2])
        bias_now = sb("b_bias_now", [P, U, 3])
        w = sb("b_w", [P, U, 3, E0])
        xg = sb("b_xg", [P, U, 2, E0])
        xgT = sb("b_xgT", [P, 2, 2 * P])
        h1 = sb("b_h1", [P, 2, 2 * P])
        h2 = sb("b_h2", [P, 2, 2 * P])
        y = sb("b_y", [P, U, 2, E0])
        ps_t = [ctx.enter_context(nc.psum_tensor(f"b_ps_t{n}", [P, 512], F32)) for n in range(2)]
        ps_x = [ctx.enter_context(nc.psum_tensor(f"b_ps_x{n}", [P, 512], F32)) for n in range(2)]
        ps_1 = [ctx.enter_context(nc.psum_tensor(f"b_ps_1{n}", [P, 512], F32)) for n in range(2)]
        ps_2 = [ctx.enter_context(nc.psum_tensor(f"b_ps_2{n}", [P, 512], F32)) for n in range(2)]

        s_pass = sem("b_pass")
        s_const = sem("b_const")
        s_ahead = sem("b_ahead")
        s_lg = sem("b_lg")
        s_w = [sem(f"b_w{u}") for u in range(U)]
        s_g = sem("b_gate_step")
        s_exp = sem("b_exp_ready")
        s_turned = sem("b_slots_turned")
        s_row = sem("b_row_at_ready")
        s_row_in = sem("b_row_in_ready")
        s_row_now = sem("b_row_now_ready", U)
        s_bias_now = sem("b_bias_now_ready", U)
        s_val_now = sem("b_val_now_ready", U)
        s_xg = [sem_from_0(f"b_xg{u}") for u in range(U)]
        s_xt_fill = sem("b_xgT_filled", U)
        s_xt = sem("b_xgT_ready", U)
        s_1_fill = sem("b_h1_filled", U)
        s_1 = sem("b_h1_ready", U)
        s_2_fill = sem("b_h2_filled", U)
        s_2 = sem("b_h2_ready", U)
        s_3_fill = sem("b_y_filled", U)
        s_y = sem("b_y_ready", U)
        s_out = [sem_from_0(f"b_y_landed{h}") for h in range(2)]
        s_added = sem("b_y_added", U)

        n_iter = NE // U
        loads = [(ident[:, :], a["c_ident"]), (row0[:, :], a["c_row0"])]
        loads += [(bias[:, n, :], a[f"L0_ffn_b{n + 1}"].rearrange("e o -> (e o)").partition_broadcast(P)) for n in range(3)]
        w_v = [a[f"L0_ffn_w{n + 1}"] for n in range(3)]
        block = ctx.enter_context(nc.Block())

        @block.sync
        def _(sp):
            sp.dma_start(lg[:, :], scr["lg"]).then_inc(s_lg, 16)
            for dst, src in loads:
                sp.dma_start(dst, src).then_inc(s_const, 16)
            for dst, src in ahead:
                sp.dma_start(dst, src).then_inc(s_ahead, 16)
            with sp.Fori(0, n_iter) as i:
                for u in range(U):
                    wait_expert(sp, s_3_fill, i * U + (u - U))
                    for n in range(3):
                        sp.dma_start(w[:, u, n], w_v[n][i * U + u]).then_inc(s_w[u], 16)
            sp.wait_ge(s_ahead, 16 * len(ahead) + 1)

        @block.vector
        def _(dve):
            step = [0]

            def then(ins):
                step[0] += 1
                ins.then_inc(s_g, 1)
                dve.wait_ge(s_g, step[0] + 1)

            dve.wait_ge(s_lg, 17)
            then(dve.tensor_reduce(mx[:, :], lg[:, :], AX.X, ALU.max))
            then(dve.tensor_scalar(nmx[:, :], mx[:, :], -1.0, None, ALU.mult))
            dve.wait_ge(s_exp, 2)
            then(dve.reciprocal(rsum[:, :], ssum[:, :]))
            then(dve.tensor_scalar(pr[:, 0], ex[:, :], rsum[:, :], None, ALU.mult))
            for r in range(TOPK // 8):
                now = slice(8 * r, 8 * r + 8)
                then(dve.max(vals[:, now], pr[:, r % 2]))
                then(dve.max_index(idx[:, now], vals[:, now], pr[:, r % 2]))
                if r + 1 < TOPK // 8:
                    then(dve.match_replace(pr[:, (r + 1) % 2], vals[:, now], pr[:, r % 2], -1.0))
            then(dve.tensor_copy(rowf[:, :], idx[:, :]))
            dve.wait_ge(s_const, 16 * len(loads) + 1)
            then(dve.tensor_scalar(rowf[:, :], rowf[:, :], row0[:, :], None, ALU.add))
            dve.wait_ge(s_turned, 2)
            for b4 in range(4):
                q = slice(32 * b4, 32 * b4 + 32)
                for src, dst in ((ps_t[0], row_at), (ps_t[1], val_at)):
                    turned = src[0:TOPK, 0:P].rearrange("k (h b e) -> k e h b", h=2, b=4)[:, :, :, b4]
                    last = dve.tensor_copy(dst[q, :, :], turned)
            last.then_inc(s_row, 1)
            dve.wait_ge(s_row, 2)
            with dve.Fori(0, n_iter) as i:
                for u in range(U):
                    e = i * U
                    wait_expert(dve, s_y, e + (u - U))
                    dve.tensor_copy(val_now[:, u, :], val_at[:, e + u]).then_inc(s_val_now, 1)
                    wait_expert(dve, s_3_fill, e + u)
                    wait_expert(dve, s_val_now, e + u)
                    wait_expert(dve, s_bias_now, e + u)
                    wait_expert(dve, s_added, e + (u - U))
                    for h in range(2):
                        last = dve.tensor_scalar(y[:, u, h], ps_x[u % 2][:, P * h:P * h + P], bias_now[:, u, 2:3],
                                                 val_now[:, u, h:h + 1], ALU.add, ALU.mult)
                    last.then_inc(s_y, 1)
        gate_steps = 4 + 3 * (TOPK // 8) - 1 + 2

        @block.gpsimd
        def _(pool):
            for s, start in semaphores:
                pool.sem_inc(s, start)
            pool.wait_ge(s_row, 2)

            def fetch(u, rows, count):
                pool.tensor_copy(row_in[:, u, :], rows).then_inc(s_row_in, 1)
                pool.wait_ge(s_row_in, count + 1)
                alone(pool, s_pass)
                for h in range(2):
                    pool.indirect_dma_start(
                        out=xg[:, u, h], out_offset=None, in_=scr["xn"],
                        in_offset=bass.IndirectOffsetOnAxis(ap=row_in[:, u, h:h + 1], axis=0)).then_inc(s_xg[u], 16)

            for u in range(U):
                fetch(u, row_at[:, u], u + 1)

            def add_outputs(i, fetch_next):
                for u in range(U):
                    e = i * U
                    pool.tensor_copy(row_now[:, u, :], row_at[:, e + u]).then_inc(s_row_now, 1)
                    if fetch_next:
                        wait_expert(pool, s_xt_fill, e + u)
                        fetch(u, row_at[:, e + (U + u)], e + (U + u + 1))
                    wait_expert(pool, s_row_now, e + u)
                    wait_expert(pool, s_y, e + u)
                    if u:
                        landed(i, u - 1)
                    alone(pool, s_pass)
                    for h in range(2):
                        pool.indirect_dma_start(
                            out=scr["x1"], out_offset=bass.IndirectOffsetOnAxis(ap=row_now[:, u, h:h + 1], axis=0),
                            in_=y[:, u, h], in_offset=None, compute_op=ALU.add).then_inc(s_out[h], 16)
                landed(i, U - 1)

            def landed(i, u):
                for h in range(2):
                    pool.wait_ge(s_out[h], i * (16 * U) + 16 * (u + 1))
                pool.sem_inc(s_added, 1)

            with pool.Fori(0, n_iter - 1) as i:
                add_outputs(i, True)
            add_outputs(n_iter - 1, False)

        @block.scalar
        def _(act):
            act.wait_ge(s_g, 3)
            act.activation(ex[:, :], lg[:, :], ACT.Exp, bias=nmx[:, :], accum_out=ssum[:, :]).then_inc(s_exp, 1)
            act.wait_ge(s_const, 16 * len(loads) + 1)
            with act.Fori(0, n_iter) as i:
                for u0 in range(0, U, 2):
                    e = i * U
                    for u in (u0, u0 + 1):
                        wait_expert(act, s_y, e + (u - U))
                        act.copy(bias_now[:, u, :], bias[:, :, e + u]).then_inc(s_bias_now, 1)
                    for u in (u0, u0 + 1):
                        wait_expert(act, s_xt_fill, e + u)
                        act.copy(xgT[:, u % 2], ps_x[u % 2][:, 0:2 * P]).then_inc(s_xt, 1)
                    wait_expert(act, s_bias_now, e + (u0 + 1))
                    for u in (u0, u0 + 1):
                        wait_expert(act, s_1_fill, e + u)
                        act.activation(h1[:, u % 2], ps_1[u % 2][:, 0:2 * P], ACT.Relu, bias=bias_now[:, u, 0:1])\
                           .then_inc(s_1, 1)
                    for u in (u0, u0 + 1):
                        wait_expert(act, s_2_fill, e + u)
                        act.activation(h2[:, u % 2], ps_2[u % 2][:, 0:2 * P], ACT.Relu, bias=bias_now[:, u, 1:2])\
                           .then_inc(s_2, 1)

        @block.tensor
        def _(pe):
            pe.wait_ge(s_g, gate_steps + 1)
            pe.transpose(ps_t[0][0:TOPK, 0:P], rowf[:, :], ident[:, :])
            pe.transpose(ps_t[1][0:TOPK, 0:P], vals[:, :], ident[:, :]).then_inc(s_turned, 1)
            with pe.Fori(0, n_iter) as i:
                for u0 in range(0, U, 2):
                    e = i * U
                    for u in (u0, u0 + 1):
                        pe.wait_ge(s_xg[u], i * 32 + 32)
                        wait_expert(pe, s_y, e + (u - 2))
                        for h in range(2):
                            last = pe.transpose(ps_x[u % 2][:, P * h:P * h + P], xg[:, u, h], ident[:, :])
                        last.then_inc(s_xt_fill, 1)
                    for u in (u0, u0 + 1):
                        wait_expert(pe, s_xt, e + u)
                        pe.wait_ge(s_w[u], i * 48 + 48 + 1)
                        pe.matmul(ps_1[u % 2][:, 0:2 * P], w[:, u, 0], xgT[:, u % 2], start=True, stop=True)\
                          .then_inc(s_1_fill, 1)
                    for u in (u0, u0 + 1):
                        wait_expert(pe, s_1, e + u)
                        pe.matmul(ps_2[u % 2][:, 0:2 * P], w[:, u, 1], h1[:, u % 2], start=True, stop=True)\
                          .then_inc(s_2_fill, 1)
                    for u in (u0, u0 + 1):
                        wait_expert(pe, s_2, e + u)
                        for h in range(2):
                            last = pe.matmul(ps_x[u % 2][:, P * h:P * h + P], h2[:, u % 2, P * h:P * h + P], w[:, u, 2],
                                             start=True, stop=True)
                        last.then_inc(s_3_fill, 1)


TABLE = [
    (("commit",),         0,    None,    0,       0,       None),
    (("g_turn",),         0,    1,       0,       None,    None),
    (("up", 0),           None, 1,       0,       1,       None),
    (("b3",),             0,    1,       None,    1,       None),
    (("norm",),           1,    None,    0,       0,       None),
    (("norm_x",),         1,    None,    None,    1,       None),
    (("norm_t",),         1,    3,       3,       None,    None),
    (("out_proj",),       None, 5,       None,    6,       None),
    (("finish",),         None, None,    None,    2,       None),
    (("down", 0),         None, 1,       None,    1,       None),
    (("up", 1),           None, 3,       3,       4,       None),
    (("gate_softmax",),   1,    None,    6,       6,       None),
    (("gate",),           1,    5,       None,    5,       None),
    (("proj",),           None, 6,       6,       None,    None),
    (("z",),              None, None,    6,       None,    None),
    (("down", 1),         None, 8,       None,    7,       None),
    (("up", 2),           None, 8,       8,       8,       None),
    (("conv",),           None, None,    None,    6,       None),
    (("split",),          None, None,    None,    None,    9),
    (("down", 2),         None, 9,       None,    9,       None),
    (("u",),              None, None,    9,       None,    None),
    (("up", 3),           None, 9,       9,       9,       None),
    (("dl",),             None, 12,      12,      None,    None),
    (("rest",),           None, None,    None,    None,    10),
    (("x_dbl",),          None, 10,      10,      None,    None),
    (("split_rest",),     None, None,    None,    None,    12),
    (("up", 4),           None, 14,      14,      14,      None),
    (("softplus",),       None, None,    13,      13,      None),
    (("down", 4),         None, 15,      None,    15,      None),
    (("down", 3),         None, 11,      None,    12,      None),
    (("join",),           None, None,    15,      None,    None),
]
PE, SCALAR, VECTOR, POOL = range(4)


def pieces(engine, d, n):
    return [piece for piece, unit, *steps in TABLE if unit in (None, d) and steps[engine] == n]


def layer1_weights(nc, ctx, a):
    def sb(name, shape):
        return ctx.enter_context(nc.sbuf_tensor(name, shape, F32))

    ident = sb("m_ident_sb", [P, P])
    sel = sb("m_sel_f", [3 * NS2, NS2])
    iota = sb("m_iota_sb", [P, NR])
    in_w = sb("m_in_w", [P, 2, 2 * DI])
    conv_w = sb("m_conv_w", [P, 2, 2, KC])
    conv_b = sb("m_conv_b", [P, 2, 2])
    x_w = sb("m_x_w", [P, 2, 2, NX])
    dt_w = sb("m_dt_w", [NX, 2, DI])
    dt_b = sb("m_dt_b", [P, 2, 2])
    a_log = sb("m_a_log", [P, 2, 2, NS])
    d_p = sb("m_d_p", [P, 2, 2])
    out_w = sb("m_out_w", [P, 2, 2, E0])
    gate_w = sb("m_gate_w", [P, NR])
    gate_b = sb("m_gate_b", [P, NR])
    w1 = sb("m_w1", [P, NX1, DH])
    w2 = sb("m_w2", [P, NX1, DH])
    w3 = sb("m_w3", [P, NX1, 2, E0])
    b1 = sb("m_b1", [P, NX1, 2])
    b2 = sb("m_b2", [P, NX1, 2])
    b3 = sb("m_b3", [NX1, E0])
    loads = [
        (ident[:, :], a["c_ident"]), (sel[:, :], a["c_sel"]), (iota[:, :], a["c_iota"]),
        (gate_w[:, :], a["L1_ffn_gate_w"]), (gate_b[:, :], a["L1_ffn_gate_b"].partition_broadcast(P)),
        (w1[:, 0:NR, :], a["L1_ffn_rw1"].rearrange("e d h -> d e h")),
        (w1[:, NR:, :], a["L1_ffn_sw1"].rearrange("e d h -> d e h")),
        (w2[:, 0:NR, :], a["L1_ffn_rw2"].rearrange("e d h -> d e h")),
        (w2[:, NR:, :], a["L1_ffn_sw2"].rearrange("e d h -> d e h")),
        (w3[:, 0:NR, :, :], a["L1_ffn_rw3"].rearrange("e (k p) d -> p e k d", p=P)),
        (w3[:, NR:, :, :], a["L1_ffn_sw3"].rearrange("e (k p) d -> p e k d", p=P)),
        (b3[0:NR, :], a["L1_ffn_rb3"]), (b3[NR:, :], a["L1_ffn_sb3"]),
        (b1[:, :, :], a["t_b1"]), (b2[:, :, :], a["t_b2"]),
    ]
    for d, s in enumerate("fb"):
        loads += [
            (in_w[:, d, :], a["t_in_w_" + s]), (conv_w[:, d], a["t_conv_w_" + s]), (conv_b[:, d], a["t_conv_b_" + s]),
            (x_w[:, d], a["t_x_w_" + s]), (dt_w[NS2:NX, d, :], a["t_dt_w_" + s]), (dt_b[:, d], a["t_dt_b_" + s]),
            (a_log[:, d], a["t_a_log_" + s]), (d_p[:, d], a["t_d_p_" + s]), (out_w[:, d], a["t_out_w_" + s]),
        ]
    named = dict(ident=ident, sel=sel, iota=iota, in_w=in_w, conv_w=conv_w, conv_b=conv_b, x_w=x_w, dt_w=dt_w, dt_b=dt_b,
                 a_log=a_log, d_p=d_p, out_w=out_w, gate_w=gate_w, gate_b=gate_b, w1=w1, w2=w2, w3=w3, b1=b1, b2=b2, b3=b3)
    return named, loads


def layer1_phase(nc, weights, scr, out):
    ctx = ExitStack()
    with ctx:
        def sb(name, shape, dt=F32):
            return ctx.enter_context(nc.sbuf_tensor(name, shape, dt))

        semaphores = []

        def sem(name, start=1):
            semaphores.append((ctx.enter_context(nc.semaphore(name)), start))
            return semaphores[-1][0]

        def ps(name):
            return ctx.enter_context(nc.psum_tensor(name, [P, 512], F32))

        w = weights
        ident, sel_f, iota, in_w, conv_w, conv_b, x_w, dt_w, dt_b, a_log, d_p, out_w = (
            w[n] for n in ("ident", "sel", "iota", "in_w", "conv_w", "conv_b", "x_w", "dt_w", "dt_b", "a_log", "d_p", "out_w"))
        gate_w, gate_b, w1, w2, w3, b1, b2, b3 = (w[n] for n in ("gate_w", "gate_b", "w1", "w2", "w3", "b1", "b2", "b3"))
        sel = sb("m_sel", [3 * NS2, NS2, P], BF16)
        a_neg = sb("m_a_neg", [P, 2, 2, NS])

        xs = sb("m_xs", [P, NC, E0])
        xn = sb("m_xn", [P, NC, E0])
        stats = sb("m_stats", [P, NC, 6])
        mv = sb("m_mv", [P, NC, 2])
        var = sb("m_var", [P, NC])
        lnv = sb("m_lnv", [P, NC])
        rstd = sb("m_rstd", [P, NC])
        xnT = sb("m_xnT", [P, T])
        xnT_x = sb("m_xnT_x", [P, T])
        gl = sb("m_gl", [P, NC, NR])
        gm = sb("m_gm", [P, NC])
        ge = sb("m_ge", [P, NC, NR])
        gs = sb("m_gs", [P, NC])
        gr = sb("m_gr", [P, NC])
        gp = sb("m_gp", [P, NC, NR])
        top = sb("m_top", [P, NC, NR])
        top_i = sb("m_top_i", [P, NC, NR], U32)
        top_f = sb("m_top_f", [P, NC, NR])
        g1 = sb("m_g1", [P, NC, NR])
        g2 = sb("m_g2", [P, NC, NR])
        g = sb("m_g", [P, NC, NX1])
        g_f = sb("m_g_f", [P, NC, NX1])
        gT = sb("m_gT", [NX1, T])
        xi = sb("m_xi", [P, 2, 2, T + 2 * (KC - 1)])
        uu = sb("m_uu", [P, 2, 2, T])
        sz = sb("m_sz", [P, 2, 2, T])
        xd = sb("m_xd", [NX, T])
        bc = sb("m_bc", [3 * NS2, 2, T], BF16)
        bc_m = sb("m_bc_m", [NS2, T], BF16)
        bc_l = sb("m_bc_l", [NS2, T], BF16)
        bc_r = sb("m_bc_r", [NS2, T])
        dl = sb("m_dl", [P, 2, T])
        sp_e = sb("m_sp_e", [P, 2, T])
        sp_w = sb("m_sp_w", [P, 2, T])
        sp_l = sb("m_sp_l", [P, 2, T])
        delta = sb("m_delta", [P, 2, 2, T])
        du = sb("m_du", [P, 2, 2, T])
        dA = sb("m_dA", [P, RING, 2, T])
        dBu = sb("m_dBu", [P, 2, 2, T])
        h = sb("m_h", [P, RING, 2, T])
        c_n = sb("m_c_n", [P, RING, T])
        hc = sb("m_hc", [P, RING, 2, T])
        s1 = sb("m_s1", [P, 2, T])
        glu = sb("m_glu", [P, 2, 2, T])
        cv = sp_w
        acc = sb("m_acc", [P, NC, E0])
        acc_p = sb("m_acc_p", [P, NC, E0])
        yo = sb("m_yo", [P, NC, E0])

        ps_y = [ps(f"m_ps_y{n}") for n in range(2)]
        ps_b = [ps(f"m_ps_b{n}") for n in range(2)]
        ps_c = ps("m_ps_c")

        def bank_uses(piece, d):
            if piece[0] == "up":
                return [(p, 5 * d + piece[1], k) for k in range(2) for p in ("p1", "p2")]
            if piece[0] == "down":
                return [("out", 5 * d + piece[1])]
            return {
                "norm_t": [("xnT",)], "gate": [("gate",)], "g_turn": [("gT",)], "b3": [("b3",)],
                "proj": [("in", 1 - d, k) for k in range(4)], "x_dbl": [("xd", 1 - d)],
                "dl": [("dl", 1 - d, k) for k in range(2)], "out_proj": [("op", 1 - d)],
            }.get(piece[0], [])

        front = ["norm", "norm_x", "norm_t", "proj", "z", "conv", "u", "x_dbl", "split", "rest", "split_rest",
                 "dl", "softplus", "join", "gate", "gate_softmax"]
        G = Banks(sem, "m_g", [ps(f"m_ps_g{n}") for n in range(3)],
                  [use for d in range(2) for n in range(NS) for piece in pieces(PE, d, n)
                   for use in bank_uses(piece, d)],
                  [use for name in front for use in bank_uses((name,), 1)])

        s_pass = sem("m_pass")
        s_setup = sem("m_setup")
        s_sel = sem("m_sel_ready")
        s_a = sem("m_a_exp")
        s_x = sem("m_x_loaded")
        s_out = sem("m_out_stored")
        s_v = sem("m_vector_step")
        s_p = sem("m_pool_step")
        s_var = sem("m_var_ready")
        s_lnv = sem("m_lnv_ready")
        s_rstd = sem("m_rstd_ready")
        s_xn = sem("m_xn_ready")
        s_gm = sem("m_gate_less_max")
        s_ge = sem("m_gate_exp")
        s_commit = sem("m_committed")
        s_xt = sem("m_xnT_x_ready")
        s_cv = sem("m_conv_ready")
        s_u = sem("m_u_ready")
        s_lo = sem("m_bc_split")
        s_bc = sem("m_bc_ready")
        s_abs = sem("m_abs_ready")
        s_e = sem("m_e_ready")
        s_l = sem("m_l_ready")
        s_delta = sem("m_delta_ready")
        s_du = sem("m_du_ready")
        s_y = sem("m_y_ready")
        s_yo = sem("m_yo_ready")
        s_o_last = sem("m_last_out_filled")
        s_b_fill = sem("m_b_filled", RING)
        s_c_fill = sem("m_c_filled", RING)
        s_c = sem("m_c_ready", RING)
        s_dA = sem("m_dA_ready", RING)
        s_dBu = sem("m_dBu_ready", RING)
        s_h = sem("m_h_ready", RING)
        s_hc = sem("m_hc_ready", RING)
        s_ysum = sem("m_ysum_done", RING - sum(summed(n) for n in range(NS - LAG, NS)))
        s_pair = sem("m_pair_added", 2)

        def wait_pair(eng, i, g):
            k = PAIRED.index(g % NS) + len(PAIRED) * (g // NS)
            eng.wait_ge(s_pair, i * (2 * len(PAIRED)) + (k + 3))

        def wait_step(eng, s, i, g):
            eng.wait_ge(s, i * NG + (g + 1 + RING))

        x_v = scr["x1"].rearrange("(b c p) e -> b p c e", b=NB, p=P)
        out_v = out.rearrange("b (c p) e -> b p c e", p=P)

        def batches(eng, which, before, step, piece):
            for name in front:
                piece(("before",), 0, name, 0, 0, 0)
            before()
            with eng.Fori(0, NB) as i:
                for d in range(2):
                    for n in range(NS):
                        step(i, d, n)
                        for name, *e in pieces(which, d, n):
                            piece((), i, name, 5 * d + e[0] if e else 1 - d, i * 2 + (d + 1), i + d)
                        step(i, d, n, True)

        block = ctx.enter_context(nc.Block())

        @block.sync
        def _(sp):
            sp.dma_start(xs[:, :, :], x_v[0]).then_inc(s_x, 16)
            with sp.Fori(0, NB) as i:
                G.wait_emptied(sp, i, "b3")
                sp.dma_start(xs[:, :, :], x_v[(i + 1) % NB]).then_inc(s_x, 16)
                sp.wait_ge(s_yo, i + 2)
                sp.dma_start(out_v[(i + NB - 1) % NB], yo[:, :, :]).then_inc(s_out, 16)
            sp.wait_ge(s_yo, NB + 2)
            sp.wait_ge(s_out, 16 * NB + 1)
            sp.dma_start(out_v[NB - 1], yo[:, :, :]).then_inc(s_out, 16)
            sp.wait_ge(s_x, 16 * (NB + 1) + 1)
            sp.wait_ge(s_out, 16 * (NB + 1) + 1)

        @block.vector
        def _(dve):
            links = [0, 0]

            def then(pre, i, ins):
                ins.then_inc(s_v, 1)
                if pre:
                    links[0] += 1
                    dve.wait_ge(s_v, links[0] + 1)
                else:
                    links[1] += 1
                    dve.wait_ge(s_v, i * V_STEPS + (V_BEFORE + links[1] + 1))

            def norm(pre, i, b):
                dve.wait_ge(s_x, b * 16 + 17)
                for c in range(NC):
                    last = dve.bn_stats(stats[:, c], xs[:, c])
                then(pre, i, last)
                alone(dve, s_pass)
                for c in range(NC):
                    last = dve.bn_aggr(mv[:, c], stats[:, c])
                then(pre, i, last)
                dve.tensor_scalar(var[:, :], mv[:, :, 1], LN_EPS, None, ALU.add).then_inc(s_var, 1)

            def norm_x(b):
                dve.wait_ge(s_rstd, b + 2)
                for c in range(NC):
                    last = dve.tensor_scalar(xn[:, c], xs[:, c], mv[:, c, 0:1], rstd[:, c:c + 1], ALU.subtract, ALU.mult)
                last.then_inc(s_xn, 1)

            def gate_less_max(pre, i):
                G.wait_filled(dve, i, *pre, "gate")
                last = dve.tensor_tensor(gl[:, :, :], G.bank(*pre, "gate")[:, 0:NC * NR].rearrange("p (c e) -> p c e", c=NC),
                                         gate_b[:, :].unsqueeze(1).broadcast_to([P, NC, NR]), ALU.add)
                G.emptied(last, *pre, "gate")
                G.wait_emptied(dve, i, *pre, "gate")
                then(pre, i, dve.tensor_reduce(gm[:, :], gl[:, :, :], AX.X, ALU.max))
                dve.tensor_tensor(gp[:, :, :], gl[:, :, :], gm[:, :].unsqueeze(2).broadcast_to([P, NC, NR]),
                                  ALU.subtract).then_inc(s_gm, 1)

            def gate_softmax(pre, i, b):
                def link(ins):
                    then(pre, i, ins)

                dve.wait_ge(s_ge, b + 2)
                link(dve.tensor_reduce(gs[:, :], ge[:, :, :], AX.X, ALU.add))
                link(dve.reciprocal(gr[:, :], gs[:, :]))
                link(dve.tensor_tensor(gp[:, :, :], ge[:, :, :], gr[:, :].unsqueeze(2).broadcast_to([P, NC, NR]), ALU.mult))
                alone(dve, s_pass)
                for c in range(NC):
                    last = dve.max(top[:, c], gp[:, c])
                link(last)
                alone(dve, s_pass)
                for c in range(NC):
                    last = dve.max_index(top_i[:, c], top[:, c], gp[:, c])
                link(last)
                link(dve.tensor_copy(top_f[:, :, :], top_i[:, :, :]))
                for c in range(NC):
                    dve.tensor_scalar(g1[:, c], iota[:, :], top_f[:, c, 0:1], top[:, c, 0:1], ALU.is_equal, ALU.mult)
                    last = dve.tensor_scalar(g2[:, c], iota[:, :], top_f[:, c, 1:2], top[:, c, 1:2], ALU.is_equal, ALU.mult)
                link(last)
                link(dve.tensor_tensor(g_f[:, :, 0:NR], g1[:, :, :], g2[:, :, :], ALU.add))

            def conv(pre, i, d, c):
                if pre:
                    dve.wait_ge(s_setup, SETUP + 1)
                for k in range(2):
                    G.wait_emptied(dve, i, *pre, "in", d, k)
                for tap in range(KC - 1, -1, -1):
                    off = tap if d == 0 else 2 * (KC - 1) - tap
                    for k in range(2):
                        src, w = xi[:, d, k, off:off + T], conv_w[:, d, k, tap:tap + 1]
                        if tap == KC - 1:
                            last = dve.tensor_scalar(cv[:, k], src, w, conv_b[:, d, k:k + 1], ALU.mult, ALU.add)
                        else:
                            last = dve.scalar_tensor_tensor(cv[:, k], src, w, cv[:, k], ALU.mult, ALU.add)
                    if tap:
                        then(pre, i, last)
                last.then_inc(s_cv, 1)

            def softplus(pre, i, d, c):
                dve.wait_ge(s_e, c + 2)
                then(pre, i, dve.tensor_scalar(sp_w[:, :, :], sp_e[:, :, :], 1.0, -1.0, ALU.add, ALU.add))
                then(pre, i, dve.tensor_tensor(sp_w[:, :, :], sp_w[:, :, :], sp_e[:, :, :], ALU.subtract))
                dve.wait_ge(s_l, c + 2)
                then(pre, i, dve.tensor_tensor(sp_w[:, :, :], sp_l[:, :, :], sp_w[:, :, :], ALU.subtract))
                flat = lambda x: x.rearrange("p k t -> p (k t)")
                dve.scalar_tensor_tensor(flat(delta[:, d]), flat(dl[:, :, :]), 0.0, flat(sp_w[:, :, :]), ALU.max, ALU.add)\
                   .then_inc(s_delta, 1)
                dve.wait_ge(s_delta, c + 2)
                dve.tensor_tensor(du[:, d], delta[:, d], uu[:, d], ALU.mult).then_inc(s_du, 1)

            def glus(i, e):
                for k in range(2):
                    G.wait_emptied(dve, i, "p1", e, k)
                    G.wait_filled(dve, i, "p2", e, k)
                    G.emptied(dve.scalar_tensor_tensor(glu[:, e % 2, k], G.bank("p2", e, k)[:, :], b2[:, e, k:k + 1],
                                                       s1[:, k], ALU.add, ALU.mult), "p2", e, k)

            def add(i, e):
                G.wait_filled(dve, i, "out", e)
                for c in range(NC):
                    last = dve.scalar_tensor_tensor(acc[:, c], G.bank("out", e)[:, P * c:P * c + P], g[:, c, e:e + 1],
                                                    acc[:, c], ALU.mult, ALU.add)
                G.emptied(last, "out", e)
                G.wait_emptied(dve, i, "out", e)

            def finish(i, d, unit):
                wait_step(dve, s_ysum, i, NS * d - 1)
                p = 1 - d
                for k in range(2):
                    last = dve.scalar_tensor_tensor(uu[:, p, k], uu[:, p, k], d_p[:, p, k:k + 1], ps_y[k][:, :],
                                                    ALU.mult, ALU.add)
                then((), i, last)
                dve.tensor_tensor(sz[:, p], uu[:, p], sz[:, p], ALU.mult).then_inc(s_y, 1)

            def add_mamba(i, d):
                G.wait_filled(dve, i, "op", 1 - d)
                o = G.bank("op", 1 - d)[:, :].rearrange("p (c n) -> p c n", c=NC)
                if d:
                    G.emptied(dve.scalar_tensor_tensor(acc[:, :, :], o, 0.5, acc[:, :, :], ALU.mult, ALU.add), "op", 0)
                    G.wait_emptied(dve, i, "op", 0)
                else:
                    dve.wait_ge(s_out, i * 16 + 1)
                    G.emptied(dve.scalar_tensor_tensor(yo[:, :, :], o, 0.5, acc_p[:, :, :], ALU.mult, ALU.add), "op", 1)
                    G.wait_emptied(dve, i, "op", 1)
                    dve.sem_inc(s_yo, 1)

            def piece(pre, i, name, d, c, b):
                if name == "norm":
                    norm(pre, i, b)
                elif name == "norm_x":
                    norm_x(b)
                    if pre:
                        dve.tensor_copy(sel[:, :, :], sel_f[:, :].unsqueeze(2).broadcast_to([3 * NS2, NS2, P]))\
                           .then_inc(s_sel, 1)
                elif name == "gate":
                    gate_less_max(pre, i)
                elif name == "gate_softmax":
                    gate_softmax(pre, i, b)
                elif name == "conv":
                    conv(pre, i, d, c)
                elif name == "softplus":
                    softplus(pre, i, d, c)
                elif name == "commit":
                    dve.tensor_copy(acc_p[:, :, :], acc[:, :, :])
                    dve.tensor_copy(g[:, :, :], g_f[:, :, :]).then_inc(s_commit, 1)
                elif name == "b3":
                    dve.wait_ge(s_commit, i + 2)
                    G.wait_filled(dve, i, "b3")
                    G.emptied(dve.tensor_tensor(acc[:, :, :], G.bank("b3")[:, :].rearrange("p (c n) -> p c n", c=NC),
                                                xs[:, :, :], ALU.add), "b3")
                    G.wait_emptied(dve, i, "b3")
                elif name == "up":
                    glus(i, d)
                elif name == "down":
                    add(i, d)
                elif name == "finish":
                    finish(i, 1 - d, c)
                elif name == "out_proj":
                    add_mamba(i, 1 - d)

            def scan(i, g):
                wait_step(dve, s_dA, i, g)
                wait_step(dve, s_dBu, i, g)
                wait_step(dve, s_hc, i, g - RING)
                t = slice(None, None, 1 if g < NS else -1)
                for b in range(2):
                    last = dve.tensor_tensor_scan(h[:, g % RING, b][:, t], dA[:, g % RING, b][:, t],
                                                  dBu[:, g % 2, b][:, t], 0.0, ALU.mult, ALU.add)
                last.then_inc(s_h, 1)

            def step(i, d, n, after=False):
                g = NS * d + n
                if not after:
                    if n == 0:
                        dve.wait_ge(s_du, i * 2 + (d + 2))
                    wait_step(dve, s_b_fill, i, g)
                    wait_step(dve, s_h, i, g - 2)
                    dve.tensor_tensor(dBu[:, g % 2], du[:, d], ps_b[g % 2][:, :].unsqueeze(1).broadcast_to([P, 2, T]),
                                      ALU.mult).then_inc(s_dBu, 1)
                    if g:
                        scan(i, g - 1)
                elif g == NG - 1:
                    scan(i, g)

            batches(dve, VECTOR, lambda: None, step, piece)
            assert links == [V_BEFORE, V_STEPS], links
            links[1] = 0
            finish(NB, 0, 0)
            dve.wait_ge(s_o_last, 2)
            dve.wait_ge(s_out, 16 * NB + 1)
            dve.scalar_tensor_tensor(yo[:, :, :], ps_y[0][:, :].rearrange("p (c n) -> p c n", c=NC), 0.5,
                                     acc[:, :, :], ALU.mult, ALU.add).then_inc(s_yo, 1)

        @block.gpsimd
        def _(pool):
            for s, start in semaphores:
                if start:
                    pool.sem_inc(s, start)
            pool.memset(xi[:, :, :, :], 0.0).then_inc(s_setup, 1)
            pool.memset(g_f[:, :, :], 0.5).then_inc(s_setup, 1)
            pool.memset(acc[:, :, :], 0.0).then_inc(s_setup, 1)
            pool.memset(uu[:, 1], 0.0).then_inc(s_setup, 1)
            pool.memset(sz[:, 1], 0.0).then_inc(s_setup, 1)
            pool.memset(hc[:, :, :, :], 0.0).then_inc(s_setup, 1)
            links = [0, 0]

            def then(pre, i, ins):
                ins.then_inc(s_p, 1)
                if pre:
                    links[0] += 1
                    pool.wait_ge(s_p, links[0] + 1)
                else:
                    links[1] += 1
                    pool.wait_ge(s_p, i * P_STEPS + (P_BEFORE + links[1] + 1))

            def piece(pre, i, name, d, c, b):
                if name == "split":
                    G.wait_emptied(pool, i, *pre, "xd", d)
                    alone(pool, s_pass)
                    then(pre, i, pool.tensor_copy(bc[0:NS2, d], xd[0:NS2, :]))
                elif name == "rest":
                    then(pre, i, pool.tensor_tensor(bc_r[:, :], xd[0:NS2, :], bc[0:NS2, d], ALU.subtract))
                elif name == "split_rest":
                    alone(pool, s_pass)
                    then(pre, i, pool.tensor_copy(bc_m[:, :], bc_r[:, :]))
                    pool.tensor_tensor(bc_l[:, :], bc_r[:, :], bc_m[:, :], ALU.subtract).then_inc(s_lo, 1)

            def step(i, d, n, after=False):
                if after:
                    return
                g = NS * d + n
                wait_step(pool, s_h, i, g)
                wait_step(pool, s_c, i, g)
                if summed((n - RING) % NS):
                    wait_step(pool, s_ysum, i, g - RING)
                else:
                    wait_pair(pool, i, g - RING + 1)
                pool.tensor_tensor(hc[:, g % RING], h[:, g % RING], c_n[:, g % RING].unsqueeze(1).broadcast_to([P, 2, T]),
                                   ALU.mult).then_inc(s_hc, 1)
                if n in PAIRED:
                    wait_step(pool, s_hc, i, g)
                    pool.tensor_tensor(hc[:, g % RING], hc[:, g % RING], hc[:, (g - 1) % RING], ALU.add).then_inc(s_pair, 1)

            batches(pool, POOL, lambda: None, step, piece)
            assert links == [P_BEFORE, P_STEPS], links

        @block.scalar
        def _(act):
            def exp_set():
                act.preload_act_table_set("natural_log_exp_and_others")

            exp_set()
            act.activation(a_neg[:, :, :, :], a_log[:, :, :, :], ACT.Exp).then_inc(s_a, 1)
            act.wait_ge(s_a, 2)
            act.mul(a_neg[:, :, :, :], a_neg[:, :, :, :], -1.0).then_inc(s_a, 1)
            act.wait_ge(s_a, 3)

            def piece(pre, i, name, d, c, b):
                if name == "norm":
                    act.wait_ge(s_var, b + 2)
                    act.activation(lnv[:, :], var[:, :], ACT.Ln).then_inc(s_lnv, 1)
                    act.wait_ge(s_lnv, b + 2)
                    act.activation(rstd[:, :], lnv[:, :], ACT.Exp, scale=-0.5).then_inc(s_rstd, 1)
                elif name == "norm_t":
                    G.wait_filled(act, i, *pre, "xnT")
                    G.emptied(act.copy(xnT[:, :], G.bank(*pre, "xnT")[:, :]), *pre, "xnT")
                elif name == "gate_softmax":
                    act.wait_ge(s_gm, b + 2)
                    act.activation(ge[:, :, :], gp[:, :, :], ACT.Exp).then_inc(s_ge, 1)
                elif name == "commit":
                    act.wait_ge(s_commit, i + 2)
                    act.copy(xnT_x[:, :], xnT[:, :]).then_inc(s_xt, 1)
                elif name == "g_turn":
                    G.wait_filled(act, i, "gT")
                    G.emptied(act.copy(gT[:, :], G.bank("gT")[0:NX1, :]), "gT")
                elif name == "proj":
                    if pre:
                        act.wait_ge(s_setup, SETUP + 1)
                    for k in range(2):
                        G.wait_filled(act, i, *pre, "in", d, k)
                        G.emptied(act.copy(xi[:, d, k, KC - 1:KC - 1 + T], G.bank(*pre, "in", d, k)[:, :]), *pre, "in", d, k)
                elif name == "z":
                    for k in range(2, 4):
                        G.wait_filled(act, i, *pre, "in", d, k)
                        G.emptied(act.activation(sz[:, d, k - 2], G.bank(*pre, "in", d, k)[:, :], ACT.Silu), *pre, "in", d, k)
                elif name == "u":
                    act.wait_ge(s_cv, c + 2)
                    act.activation(uu[:, d], cv[:, :, :], ACT.Silu).then_inc(s_u, 1)
                    if pre:
                        exp_set()
                elif name == "up":
                    for k in range(2):
                        G.wait_filled(act, i, "p1", d, k)
                        if d:
                            G.wait_emptied(act, i, "p2", d - 1, k)
                        G.emptied(act.activation(s1[:, k], G.bank("p1", d, k)[:, :], ACT.Silu, bias=b1[:, d, k:k + 1]),
                                  "p1", d, k)
                    exp_set()
                elif name == "x_dbl":
                    G.wait_filled(act, i, *pre, "xd", d)
                    G.emptied(act.copy(xd[:, :], G.bank(*pre, "xd", d)[0:NX, :]), *pre, "xd", d)
                elif name == "dl":
                    for k in range(2):
                        G.wait_filled(act, i, *pre, "dl", d, k)
                        G.emptied(act.activation(dl[:, k], G.bank(*pre, "dl", d, k)[:, :], ACT.Identity,
                                                 bias=dt_b[:, d, k:k + 1]), *pre, "dl", d, k)
                    for k in range(2):
                        G.wait_emptied(act, i, *pre, "dl", d, k)
                    act.activation(sp_l[:, :, :], dl[:, :, :], ACT.Abs).then_inc(s_abs, 1)
                    act.wait_ge(s_abs, c + 2)
                    act.activation(sp_e[:, :, :], sp_l[:, :, :], ACT.Exp, scale=-1.0).then_inc(s_e, 1)
                elif name == "softplus":
                    act.wait_ge(s_e, c + 2)
                    act.activation(sp_l[:, :, :], sp_e[:, :, :], ACT.Ln, bias=1.0).then_inc(s_l, 1)
                elif name == "join":
                    act.wait_ge(s_lo, c + 2)
                    act.copy(bc[NS2:2 * NS2, d], bc_m[:, :])
                    act.copy(bc[2 * NS2:, d], bc_l[:, :]).then_inc(s_bc, 1)

            def step(i, d, n, after=False):
                if after:
                    return
                g = NS * d + n
                if n == 0:
                    act.wait_ge(s_delta, i * 2 + (d + 2))
                wait_step(act, s_h, i, g - RING)
                for b in range(2):
                    last = act.activation(dA[:, g % RING, b], delta[:, d, b], ACT.Exp, scale=a_neg[:, d, b, n:n + 1])
                last.then_inc(s_dA, 1)
                wait_step(act, s_c_fill, i, g)
                wait_step(act, s_hc, i, g - RING)
                act.copy(c_n[:, g % RING], ps_c[:, :]).then_inc(s_c, 1)

            batches(act, SCALAR, lambda: None, step, piece)

        @block.tensor
        def _(pe):
            def piece(pre, i, name, d, c, b):
                if name == "norm_t":
                    pe.wait_ge(s_xn, b + 2)
                    G.wait_free(pe, i, *pre, "xnT")
                    for t in range(NC):
                        last = pe.transpose(G.bank(*pre, "xnT")[:, P * t:P * t + P], xn[:, t], ident[:, :])
                    G.filled(last, *pre, "xnT")
                elif name == "gate":
                    G.wait_emptied(pe, i, *pre, "xnT")
                    G.wait_free(pe, i, *pre, "gate")
                    for t in range(NC):
                        last = pe.matmul(G.bank(*pre, "gate")[:, NR * t:NR * t + NR], xnT[:, P * t:P * t + P], gate_w[:, :],
                                         start=True, stop=True)
                    G.filled(last, *pre, "gate")
                elif name == "proj":
                    if pre:
                        G.wait_emptied(pe, i, *pre, "xnT")
                    for k in range(4):
                        G.wait_free(pe, i, *pre, "in", d, k)
                        G.filled(pe.matmul(G.bank(*pre, "in", d, k)[:, :], in_w[:, d, P * k:P * k + P], xnT[:, :],
                                           start=True, stop=True), *pre, "in", d, k)
                elif name == "g_turn":
                    pe.wait_ge(s_commit, i + 2)
                    G.wait_free(pe, i, "gT")
                    for t in range(NC):
                        last = pe.transpose(G.bank("gT")[0:NX1, P * t:P * t + P], g[:, t], ident[:, :])
                    G.filled(last, "gT")
                elif name == "b3":
                    G.wait_emptied(pe, i, "gT")
                    G.wait_free(pe, i, "b3")
                    for t in range(NC):
                        last = pe.matmul(G.bank("b3")[:, P * t:P * t + P], gT[:, P * t:P * t + P], b3[:, :],
                                         start=True, stop=True)
                    G.filled(last, "b3")
                elif name == "up":
                    pe.wait_ge(s_xt, i + 2)
                    for k in range(2):
                        for p, w in (("p1", w1), ("p2", w2)):
                            G.wait_free(pe, i, p, d, k)
                            G.filled(pe.matmul(G.bank(p, d, k)[:, :], w[:, d, P * k:P * k + P], xnT_x[:, :],
                                               start=True, stop=True), p, d, k)
                elif name == "down":
                    G.wait_free(pe, i, "out", d)
                    G.wait_emptied(pe, i, "p2", d, 0)
                    G.wait_emptied(pe, i, "p2", d, 1)
                    for t in range(NC):
                        for k in range(2):
                            last = pe.matmul(G.bank("out", d)[:, P * t:P * t + P], glu[:, d % 2, k, P * t:P * t + P],
                                             w3[:, d, k, :], start=(k == 0), stop=(k == 1))
                    G.filled(last, "out", d)
                elif name == "x_dbl":
                    pe.wait_ge(s_u, c + 2)
                    G.wait_free(pe, i, *pre, "xd", d)
                    for k in range(2):
                        last = pe.matmul(G.bank(*pre, "xd", d)[0:NX, :], x_w[:, d, k, :], uu[:, d, k],
                                         start=(k == 0), stop=(k == 1))
                    G.filled(last, *pre, "xd", d)
                elif name == "dl":
                    G.wait_emptied(pe, i, *pre, "xd", d)
                    for k in range(2):
                        G.wait_free(pe, i, *pre, "dl", d, k)
                        alone(pe, s_pass)
                        G.filled(pe.matmul(G.bank(*pre, "dl", d, k)[:, :], dt_w[NS2:NX, d, P * k:P * k + P], xd[NS2:NX, :],
                                           start=True, stop=True), *pre, "dl", d, k)
                elif name == "out_proj":
                    pe.wait_ge(s_y, c + 1)
                    G.wait_free(pe, i, "op", d)
                    out_proj(G.bank("op", d), d, d).then_inc(G.fill[G.at[("op", d)][0]], 1)

            def out_proj(bank, d, only):
                for t in range(NC):
                    for k in range(2):
                        last = pe.matmul(bank[:, P * t:P * t + P], sz[:, d, k, P * t:P * t + P], out_w[:, d, k, :],
                                         start=(k == 0), stop=(k == 1))
                return last

            def y_sum(i, g):
                count = summed(g % NS)
                if count == 0:
                    return
                if count == 2:
                    wait_pair(pe, i, g)
                else:
                    wait_step(pe, s_hc, i, g)
                first = g % NS < 2 and g % NS + 1 == count
                if first and g >= 0:
                    pe.wait_ge(s_y, i * 2 + (g // NS + 2))
                for b in range(2):
                    ins = pe.matmul(ps_y[b][:, :], ident[:, :], hc[:, g % RING, b], start=first, stop=g in (NS - 1, -1))
                ins.then_inc(s_ysum, count)

            def step(i, d, n, after=False):
                g = NS * d + n
                if after:
                    if n >= LAG:
                        y_sum(i, g - LAG)
                    return
                if n == 0:
                    pe.wait_ge(s_bc, i * 2 + (d + 2))
                wait_step(pe, s_dBu, i, g - 2)
                pe.matmul(ps_b[g % 2][:, :], sel[:, n, :], bc[:, d], start=True, stop=True).then_inc(s_b_fill, 1)
                wait_step(pe, s_c, i, g - 1)
                pe.matmul(ps_c[:, :], sel[:, n + NS, :], bc[:, d], start=True, stop=True).then_inc(s_c_fill, 1)
                if n < LAG:
                    y_sum(i, g - LAG)

            def before():
                pe.wait_ge(s_setup, SETUP + 1)
                pe.wait_ge(s_sel, 2)
                for b in range(2):
                    pe.matmul(ps_y[b][:, :], ident[:, :], hc[:, 0, b], start=True, stop=False)

            batches(pe, PE, before, step, piece)
            for late in range(-LAG, 0):
                y_sum(NB, late)
            pe.wait_ge(s_y, NB * 2 + 2)
            out_proj(ps_y[0], 1, 1).then_inc(s_o_last, 1)


def build(nc, a, out):
    scr = {
        "xn": nc.dram_tensor("scratch_xn", (NB * T, E0), F32).ap(),
        "lg": nc.dram_tensor("scratch_lg", (NB * NE, T), F32).ap(),
        "x1": nc.dram_tensor("scratch_x1", (NB * T, E0), F32).ap(),
    }
    with ExitStack() as ctx:
        weights, loads = layer1_weights(nc, ctx, a)
        attention_phase(nc, a, scr)
        expert_phase(nc, a, scr, loads)
        layer1_phase(nc, weights, scr, out)


def kernel(**inputs):
    import concourse.bacc as _bacc
    from concourse.bass_utils import run_bass_kernel_spmd as _run

    arrays = {k: np.ascontiguousarray(v) for k, v in inputs.items()}
    arrays.update(layouts(arrays))
    arrays.update(constants())
    unused = {f"L1_attn_{k}_{s}" for s in "fb"
              for k in ("inW", "convW", "convB", "xpW", "dtW", "dtB", "Alog", "Dp", "outW")}
    unused |= {"L1_ffn_rb1", "L1_ffn_rb2", "L1_ffn_sb1", "L1_ffn_sb2"}
    arrays = {k: v for k, v in arrays.items() if k not in unused}
    nc = _bacc.Bacc("TRN2", target_bir_lowering=False, num_devices=1)
    a = {k: nc.dram_tensor("in_" + k, v.shape, mybir.dt.from_np(v.dtype), kind="ExternalInput").ap()
         for k, v in arrays.items()}
    out = nc.dram_tensor("out", (NB, T, E0), F32, kind="ExternalOutput").ap()
    build(nc, a, out)
    r = _run(nc, [{"in_" + k: v for k, v in arrays.items()}], core_ids=[0])
    return r.results[0]["out"]
```
